# Optimizing a Trainium2 kernel written in Bass

```python
import numpy as np
import jax
import jax.numpy as jnp

def _softmax(x, axis=-1):
    return jax.nn.softmax(x, axis=axis)

def _gelu(x):
    return jax.nn.gelu(x, approximate=True)

def _silu(x):
    return jax.nn.silu(x)

def _sigmoid(x):
    return jax.nn.sigmoid(x)

def _layernorm(x, axis=-1, eps=1e-05):
    m = jnp.mean(x, axis=axis, keepdims=True)
    v = jnp.var(x, axis=axis, keepdims=True)
    return (x - m) / jnp.sqrt(v + eps)

def _scatter_add(tgt, idx, src, axis=0):
    return tgt.at[idx].add(src)

def _segment_sum(src, seg, n):
    return jax.ops.segment_sum(src, seg, n)
kernel_name = 'mk_prb_d2_jaxref_r8_93bf14'

def setup_inputs(seed: int=0):
    np.random.seed(seed)
    _w = jnp.asarray

    def _L0_attn_setup():
        import jax, jax.numpy as jnp
        import numpy as np
        HIDDEN = 128
        NUM_HEADS = 16
        NUM_KV = 4
        HEAD_DIM = HIDDEN // NUM_HEADS
        GROUPS = NUM_HEADS // NUM_KV
        SCALE = HEAD_DIM ** 0.5
        key = jax.random.key(seed)
        ks = jax.random.split(key, 9)
        s = 0.02
        B, N = (4, 256)
        return {'x': jax.random.normal(ks[0], (B, N, HIDDEN), dtype=jnp.float32), 'Wq': jax.random.normal(ks[1], (HIDDEN, NUM_HEADS * HEAD_DIM), dtype=jnp.float32) * s, 'bq': jnp.zeros((NUM_HEADS * HEAD_DIM,), dtype=jnp.float32), 'Wk': jax.random.normal(ks[2], (HIDDEN, NUM_KV * HEAD_DIM), dtype=jnp.float32) * s, 'bk': jnp.zeros((NUM_KV * HEAD_DIM,), dtype=jnp.float32), 'Wv': jax.random.normal(ks[3], (HIDDEN, NUM_KV * HEAD_DIM), dtype=jnp.float32) * s, 'bv': jnp.zeros((NUM_KV * HEAD_DIM,), dtype=jnp.float32), 'Wo': jax.random.normal(ks[4], (NUM_HEADS * HEAD_DIM, HIDDEN), dtype=jnp.float32) * s, 'bo': jnp.zeros((HIDDEN,), dtype=jnp.float32)}
    _L0_attn_in = _L0_attn_setup()

    def _L0_ffn_setup():
        import jax, jax.numpy as jnp
        import numpy as np
        B, T, D = (1, 256, 128)
        E, DFF = (8, 512)

        def _gating(logits):
            S, num_e = logits.shape
            gates = jax.nn.softmax(logits.astype(jnp.float32), axis=1)
            idx1 = jnp.argmax(gates, axis=1)
            mask1 = jax.nn.one_hot(idx1, num_e, dtype=jnp.int32)
            logits_ex1 = jnp.where(mask1.astype(bool), -jnp.inf, logits)
            idx2 = jnp.argmax(logits_ex1, axis=1)
            mask2 = jax.nn.one_hot(idx2, num_e, dtype=jnp.int32)
            loc1 = jnp.cumsum(mask1, axis=0) - 1
            loc2 = jnp.cumsum(mask2, axis=0) - 1 + jnp.sum(mask1, axis=0, keepdims=True)
            loc1_s = jnp.sum(loc1 * mask1, axis=1)
            loc2_s = jnp.sum(loc2 * mask2, axis=1)
            g1 = jnp.sum(gates * mask1, axis=1)
            g2 = jnp.sum(gates * mask2, axis=1)
            denom = jnp.maximum(g1 + g2, jnp.finfo(jnp.float32).eps)
            g1, g2 = (g1 / denom, g2 / denom)
            cap = S
            loc1_sc = jax.nn.one_hot(loc1_s, cap, dtype=jnp.float32)
            loc2_sc = jax.nn.one_hot(loc2_s, cap, dtype=jnp.float32)
            combine = (g1[:, None] * mask1)[:, :, None] * loc1_sc[:, None, :] + (g2[:, None] * mask2)[:, :, None] * loc2_sc[:, None, :]
            dispatch_mask = combine != 0
            return (combine.astype(logits.dtype), dispatch_mask)
        key = jax.random.key(seed)
        k1, k2, k3, k4 = jax.random.split(key, 4)
        x = jax.random.normal(k1, (B, T, D), dtype=jnp.float32)
        Wg = jax.random.normal(k2, (D, E), dtype=jnp.float32) * (1.0 / np.sqrt(D))
        w1 = jax.random.normal(k3, (D, DFF), dtype=jnp.float32) * (1.0 / np.sqrt(D))
        w2 = jax.random.normal(k4, (DFF, D), dtype=jnp.float32) * (1.0 / np.sqrt(DFF))
        return {'x': x, 'Wg': Wg, 'w1': w1, 'w2': w2}
    _L0_ffn_in = _L0_ffn_setup()

    def _L1_attn_setup():
        import jax, jax.numpy as jnp
        import numpy as np
        D_MODEL, D_STATE, D_CONV, EXPAND = (128, 16, 4, 2)
        D_INNER = EXPAND * D_MODEL
        BATCH, SEQ = (4, 512)
        DT_MIN, DT_MAX = (0.001, 0.1)
        key = jax.random.key(seed)
        ks = jax.random.split(key, 7)
        s = 0.02
        x = jax.random.normal(ks[0], (BATCH, SEQ, D_MODEL), jnp.float32)
        W_in = jax.random.normal(ks[1], (D_MODEL, 2 * D_INNER), jnp.float32) * s
        conv_w = jax.random.normal(ks[2], (D_INNER, 1, D_CONV), jnp.float32) * 0.3
        conv_b = jnp.zeros((D_INNER,), jnp.float32)
        A_log = jnp.log(jnp.arange(1, D_STATE + 1, dtype=jnp.float32) * jnp.pi) + DT_MIN
        A_log = jnp.broadcast_to(A_log[None, :], (D_INNER, D_STATE)).copy()
        D = jnp.ones((D_INNER,), jnp.float32).at[::2].set(-1.0)
        W_x = jax.random.normal(ks[3], (D_INNER, D_STATE), jnp.float32) * s
        W_dt = jax.random.normal(ks[4], (D_INNER, D_INNER), jnp.float32) * s
        dt = jnp.exp(jax.random.uniform(ks[5], (D_INNER,)) * (np.log(DT_MAX) - np.log(DT_MIN)) + np.log(DT_MIN))
        b_dt = dt + jnp.log(-jnp.expm1(-dt))
        W_out = jax.random.normal(ks[6], (D_INNER, D_MODEL), jnp.float32) * s
        return dict(x=x, W_in=W_in, conv_w=conv_w, conv_b=conv_b, A_log=A_log, D=D, W_x=W_x, W_dt=W_dt, b_dt=b_dt, W_out=W_out)
    _L1_attn_in = _L1_attn_setup()

    def _L1_ffn_setup():
        import jax, jax.numpy as jnp
        import numpy as np
        D_IN, D_HID = (128, 512)

        def _ternary(key, shape):
            return jax.random.randint(key, shape, -1, 2).astype(jnp.float32)

        def _tlin(x, w, s):
            return jnp.einsum('bsi,oi->bso', x, w) * s
        key = jax.random.key(seed)
        ks = jax.random.split(key, 12)
        inv = lambda fan: 1.0 / np.sqrt(fan).astype(np.float32)
        return {'x': jax.random.normal(ks[0], (4, 256, D_IN), dtype=jnp.float32), 'w1_w': _ternary(ks[1], (D_HID, D_IN)), 'w1_s': jax.random.uniform(ks[2], (D_HID,), dtype=jnp.float32) * inv(D_IN), 'w2_w': _ternary(ks[3], (D_HID, D_IN)), 'w2_s': jax.random.uniform(ks[4], (D_HID,), dtype=jnp.float32) * inv(D_IN), 'h1_w': _ternary(ks[5], (D_HID, D_HID)), 'h1_s': jax.random.uniform(ks[6], (D_HID,), dtype=jnp.float32) * inv(D_HID), 'h2_w': _ternary(ks[7], (D_HID, D_HID)), 'h2_s': jax.random.uniform(ks[8], (D_HID,), dtype=jnp.float32) * inv(D_HID), 'w3_w': _ternary(ks[9], (D_IN, D_HID)), 'w3_s': jax.random.uniform(ks[10], (D_IN,), dtype=jnp.float32) * inv(D_HID)}
    _L1_ffn_in = _L1_ffn_setup()
    _d = {'L0_attn_x': _L0_attn_in['x'], 'L0_attn_Wq': _L0_attn_in['Wq'], 'L0_attn_bq': _L0_attn_in['bq'], 'L0_attn_Wk': _L0_attn_in['Wk'], 'L0_attn_bk': _L0_attn_in['bk'], 'L0_attn_Wv': _L0_attn_in['Wv'], 'L0_attn_bv': _L0_attn_in['bv'], 'L0_attn_Wo': _L0_attn_in['Wo'], 'L0_attn_bo': _L0_attn_in['bo'], 'L0_ffn_Wg': _L0_ffn_in['Wg'], 'L0_ffn_w1': _L0_ffn_in['w1'], 'L0_ffn_w2': _L0_ffn_in['w2'], 'L1_attn_W_in': _L1_attn_in['W_in'], 'L1_attn_conv_w': _L1_attn_in['conv_w'], 'L1_attn_conv_b': _L1_attn_in['conv_b'], 'L1_attn_A_log': _L1_attn_in['A_log'], 'L1_attn_D': _L1_attn_in['D'], 'L1_attn_W_x': _L1_attn_in['W_x'], 'L1_attn_W_dt': _L1_attn_in['W_dt'], 'L1_attn_b_dt': _L1_attn_in['b_dt'], 'L1_attn_W_out': _L1_attn_in['W_out'], 'L1_ffn_w1_w': _L1_ffn_in['w1_w'], 'L1_ffn_w1_s': _L1_ffn_in['w1_s'], 'L1_ffn_w2_w': _L1_ffn_in['w2_w'], 'L1_ffn_w2_s': _L1_ffn_in['w2_s'], 'L1_ffn_h1_w': _L1_ffn_in['h1_w'], 'L1_ffn_h1_s': _L1_ffn_in['h1_s'], 'L1_ffn_h2_w': _L1_ffn_in['h2_w'], 'L1_ffn_h2_s': _L1_ffn_in['h2_s'], 'L1_ffn_w3_w': _L1_ffn_in['w3_w'], 'L1_ffn_w3_s': _L1_ffn_in['w3_s']}
    _x0 = _d['L0_attn_x']
    _d['L0_attn_x'] = jax.random.normal(jax.random.fold_in(jax.random.key(seed), 1), (8, 256, 128), dtype=_x0.dtype)
    del _x0
    return _d

def reference(L0_attn_x, L0_attn_Wq, L0_attn_bq, L0_attn_Wk, L0_attn_bk, L0_attn_Wv, L0_attn_bv, L0_attn_Wo, L0_attn_bo, L0_ffn_Wg, L0_ffn_w1, L0_ffn_w2, L1_attn_W_in, L1_attn_conv_w, L1_attn_conv_b, L1_attn_A_log, L1_attn_D, L1_attn_W_x, L1_attn_W_dt, L1_attn_b_dt, L1_attn_W_out, L1_ffn_w1_w, L1_ffn_w1_s, L1_ffn_w2_w, L1_ffn_w2_s, L1_ffn_h1_w, L1_ffn_h1_s, L1_ffn_h2_w, L1_ffn_h2_s, L1_ffn_w3_w, L1_ffn_w3_s):

    def _L0_attn_ref(x, Wq, bq, Wk, bk, Wv, bv, Wo, bo):
        import jax, jax.numpy as jnp
        import numpy as np
        HIDDEN = 128
        NUM_HEADS = 16
        NUM_KV = 4
        HEAD_DIM = HIDDEN // NUM_HEADS
        GROUPS = NUM_HEADS // NUM_KV
        SCALE = HEAD_DIM ** 0.5
        B, N, _ = x.shape
        q = x @ Wq + bq
        k = x @ Wk + bk
        v = x @ Wv + bv
        q = q.reshape(B, N, NUM_HEADS, HEAD_DIM).transpose(0, 2, 1, 3)
        q = q.reshape(B, NUM_KV, GROUPS, N, HEAD_DIM).transpose(0, 2, 1, 3, 4)
        k = k.reshape(B, N, NUM_KV, HEAD_DIM).transpose(0, 2, 1, 3)
        v = v.reshape(B, N, NUM_KV, HEAD_DIM).transpose(0, 2, 1, 3)
        scores = jnp.einsum('bghnd,bhsd->bghns', q, k)
        attn = jax.nn.softmax(scores / SCALE, axis=-1)
        out = jnp.einsum('bghns,bhsd->bghnd', attn, v)
        out = out.transpose(0, 3, 1, 2, 4).reshape(B, N, NUM_HEADS * HEAD_DIM)
        return out @ Wo + bo

    def _L0_ffn_ref(x, Wg, w1, w2):
        import jax, jax.numpy as jnp
        import numpy as np
        B, T, D = (1, 256, 128)
        E, DFF = (8, 512)

        def _gating(logits):
            S, num_e = logits.shape
            gates = jax.nn.softmax(logits.astype(jnp.float32), axis=1)
            idx1 = jnp.argmax(gates, axis=1)
            mask1 = jax.nn.one_hot(idx1, num_e, dtype=jnp.int32)
            logits_ex1 = jnp.where(mask1.astype(bool), -jnp.inf, logits)
            idx2 = jnp.argmax(logits_ex1, axis=1)
            mask2 = jax.nn.one_hot(idx2, num_e, dtype=jnp.int32)
            loc1 = jnp.cumsum(mask1, axis=0) - 1
            loc2 = jnp.cumsum(mask2, axis=0) - 1 + jnp.sum(mask1, axis=0, keepdims=True)
            loc1_s = jnp.sum(loc1 * mask1, axis=1)
            loc2_s = jnp.sum(loc2 * mask2, axis=1)
            g1 = jnp.sum(gates * mask1, axis=1)
            g2 = jnp.sum(gates * mask2, axis=1)
            denom = jnp.maximum(g1 + g2, jnp.finfo(jnp.float32).eps)
            g1, g2 = (g1 / denom, g2 / denom)
            cap = S
            loc1_sc = jax.nn.one_hot(loc1_s, cap, dtype=jnp.float32)
            loc2_sc = jax.nn.one_hot(loc2_s, cap, dtype=jnp.float32)
            combine = (g1[:, None] * mask1)[:, :, None] * loc1_sc[:, None, :] + (g2[:, None] * mask2)[:, :, None] * loc2_sc[:, None, :]
            dispatch_mask = combine != 0
            return (combine.astype(logits.dtype), dispatch_mask)
        d_model = x.shape[2]
        xs = x.reshape(-1, d_model)
        logits = xs @ Wg
        combine, dispatch_mask = _gating(logits)
        dispatched = jnp.einsum('sec,sm->ecm', dispatch_mask.astype(jnp.float32), xs)
        expert_out = jax.nn.relu(dispatched @ w1) @ w2
        out = jnp.einsum('sec,ecm->sm', combine, expert_out)
        return out.reshape(x.shape)

    def _L1_attn_ref(x, W_in, conv_w, conv_b, A_log, D, W_x, W_dt, b_dt, W_out):
        import jax, jax.numpy as jnp
        import numpy as np
        D_MODEL, D_STATE, D_CONV, EXPAND = (128, 16, 4, 2)
        D_INNER = EXPAND * D_MODEL
        BATCH, SEQ = (4, 512)
        DT_MIN, DT_MAX = (0.001, 0.1)
        B, L, _ = x.shape
        d_inner = W_in.shape[1] // 2
        K = conv_w.shape[-1]
        xz = x @ W_in
        xs, z = (xz[..., :d_inner], xz[..., d_inner:])
        xc = jax.lax.conv_general_dilated(xs.transpose(0, 2, 1), conv_w, window_strides=(1,), padding=[(K - 1, 0)], feature_group_count=d_inner, dimension_numbers=('NCH', 'OIH', 'NCH'))
        xc = xc + conv_b[None, :, None]
        xs = jax.nn.silu(xc.transpose(0, 2, 1))
        dt = jax.nn.softplus(xs @ W_dt + b_dt)
        Bs = xs @ W_x
        A_exp = jnp.exp(A_log)

        def step(h, inp):
            dt_t, Bs_t, x_t = inp
            h = h * jnp.exp(-A_exp[None] * dt_t[..., None]) + Bs_t[:, None, :]
            return (h, jnp.sum(h, axis=-1) + D * x_t)
        h0 = jnp.zeros((B, d_inner, A_exp.shape[1]), x.dtype)
        _, ys = jax.lax.scan(step, h0, (dt.transpose(1, 0, 2), Bs.transpose(1, 0, 2), xs.transpose(1, 0, 2)))
        y = ys.transpose(1, 0, 2) * jax.nn.silu(z)
        return y @ W_out

    def _L1_ffn_ref(x, w1_w, w1_s, w2_w, w2_s, h1_w, h1_s, h2_w, h2_s, w3_w, w3_s):
        import jax, jax.numpy as jnp
        import numpy as np
        D_IN, D_HID = (128, 512)

        def _ternary(key, shape):
            return jax.random.randint(key, shape, -1, 2).astype(jnp.float32)

        def _tlin(x, w, s):
            return jnp.einsum('bsi,oi->bso', x, w) * s
        h = jax.nn.silu(_tlin(x, w1_w, w1_s)) * _tlin(x, w2_w, w2_s)
        h = jax.nn.gelu(_tlin(h, h1_w, h1_s), approximate=False)
        h = jax.nn.gelu(_tlin(h, h2_w, h2_s), approximate=False)
        return _tlin(h, w3_w, w3_s)
    x = L0_attn_x
    xn = _layernorm(x, axis=-1)
    x = x + _L0_attn_ref(xn, L0_attn_Wq, L0_attn_bq, L0_attn_Wk, L0_attn_bk, L0_attn_Wv, L0_attn_bv, L0_attn_Wo, L0_attn_bo) + _L0_ffn_ref(xn, L0_ffn_Wg, L0_ffn_w1, L0_ffn_w2)
    xn = _layernorm(x, axis=-1)
    x = x + _L1_attn_ref(xn, L1_attn_W_in, L1_attn_conv_w, L1_attn_conv_b, L1_attn_A_log, L1_attn_D, L1_attn_W_x, L1_attn_W_dt, L1_attn_b_dt, L1_attn_W_out) + _L1_ffn_ref(xn, L1_ffn_w1_w, L1_ffn_w1_s, L1_ffn_w2_w, L1_ffn_w2_s, L1_ffn_h1_w, L1_ffn_h1_s, L1_ffn_h2_w, L1_ffn_h2_s, L1_ffn_w3_w, L1_ffn_w3_s)
    return x

_drawn_inputs = setup_inputs


def setup_inputs(seed=0):
    import zlib

    import numpy as np

    out = dict(_drawn_inputs(seed))
    spreads = {'L0_attn_bq': (0.0, 0.1),
     'L0_attn_bk': (0.0, 0.1),
     'L0_attn_bv': (0.0, 0.1),
     'L0_attn_bo': (0.0, 0.1),
     'L1_attn_conv_b': (0.0, 0.1)}
    factors = {}
    for name, (base, spread) in spreads.items():
        noise = np.random.default_rng([zlib.crc32(name.encode()), seed]).standard_normal(out[name].shape)
        drawn = base * np.exp(spread * noise) if base else spread * noise
        out[name] = jnp.asarray(drawn.astype(out[name].dtype))
    for name, factor in factors.items():
        out[name] = (out[name] * factor).astype(out[name].dtype)
    return out
```

```python
from contextlib import ExitStack

import numpy as np

import concourse.bass as bass
from concourse import mybir

F32, BF16 = mybir.dt.float32, mybir.dt.bfloat16
ALU, ACT, AX = mybir.AluOpType, mybir.ActivationFunctionType, mybir.AxisListType

P = 128
NB, T = 8, 256
NT = NB * T // P
TPB = T // P
NH, NKV, HD = 16, 4, 8
G = NH // NKV
NE = 8
DFF = 512
KC = DFF // P
DI = 256
CI = DI // P
NS = 16
TAPS = 4
GT = 512
NG = NB * T // GT
GB = GT // T
GTT = GT // P
LN_EPS = 1e-5
F32_EPS = float(np.finfo(np.float32).eps)
Q_PART = [0, 0, 0, 1, 1, 2]
K_PART = [0, 1, 2, 0, 1, 0]
NPART = 3
ROWS = HD * len(Q_PART)
MROWS = ROWS + NPART
VW = 32


def reached(eng, sem, b, per, k):
    v = b * per + k
    if isinstance(v, int) and v <= 0:
        return
    eng.wait_ge(sem, v)


def settled(eng, sem, v):
    eng.wait_ge(sem, v)


def layer0(nc, a, w, t, done):
    ctx = ExitStack()
    with ctx:
        def sb(name, shape, dt=F32):
            return ctx.enter_context(nc.sbuf_tensor(name, shape, dt))

        def sem(name):
            return ctx.enter_context(nc.semaphore(name))

        def bank(name):
            return ctx.enter_context(nc.psum_tensor(name, [P, 512], F32))

        x_sb, xb_sb = sb("x_sb", [P, NT, P]), sb("xb_sb", [P, NT, P])
        bo_bc, bv_bc = sb("bo_bc", [P, P]), sb("bv_bc", [P, NKV * HD])
        wq, wk4, wv = sb("wq", [P, P]), sb("wk4", [P, 4, NKV * HD]), sb("wv", [P, NKV * HD])
        wo, wg = sb("wo", [P, P]), sb("wg", [P, NE])
        w1, w2 = sb("w1", [P, DFF]), sb("w2", [P, KC, P])
        bq_c, bk_c = sb("bq_c", [P, 1]), sb("bk_c", [P, 1])
        bst, mv = sb("bst", [P, NT, 6]), sb("mv", [P, NT, 2])
        std, rstd = sb("std", [P, NT]), sb("rstd", [P, NT])
        xn = sb("xn", [P, TPB, P])
        xnT = [sb(f"xnT{p}", [P, T]) for p in range(2)]
        qk = sb("qk", [P, 2 * T])
        qk_rest = sb("qk_rest", [P, 2 * T])
        qk_parts = sb("qk_parts", [P, NPART, 2 * T], BF16)
        q_st = [sb(f"q_st{p}", [MROWS, NH, T], BF16) for p in range(2)]
        k_st = [sb(f"k_st{p}", [MROWS, NKV, T], BF16) for p in range(2)]
        v_sb = [sb(f"v_sb{p}", [P, TPB, NKV, VW]) for p in range(2)]
        mx = sb("mx", [P, NH, TPB])
        negm, negm_rest = sb("negm", [TPB * NH, P]), sb("negm_rest", [TPB * NH, P])
        m_parts = sb("m_parts", [TPB * NH, NPART, P], BF16)
        pt = sb("pt", [P, 8, 512])
        o_sb = sb("o_sb", [P, 2, 512])
        on = sb("on", [P, TPB, P])
        rden = sb("rden", [P, 2, 16])
        oT = sb("oT", [P, T])
        hT = sb("hT", [P, KC, T])
        srt, gex = sb("srt", [P, TPB, NE]), sb("gex", [P, TPB, NE])
        gd, g4, g2 = sb("gd", [P, TPB, NE]), sb("g4", [P, TPB, 4]), sb("g2", [P, TPB, 2])
        gz, gp2, gs = sb("gz", [P, TPB, 1]), sb("gp2", [P, TPB, 2]), sb("gs", [P, TPB, 1])
        grz, grm = sb("grz", [P, TPB, 1]), sb("grm", [P, TPB, 1])
        gm, gq, gate = sb("gm", [P, TPB, 1]), sb("gq", [P, TPB, 2]), sb("gate", [P, TPB, 1])
        ident, x1 = t["ident"], t["x1"]

        s_bank = [bank(f"s_bank{i}") for i in range(2)]
        st_bank = [bank(f"st_bank{i}") for i in range(2)]
        pv_bank = bank("pv_bank")
        bA, bB, bC = bank("bA"), bank("bB"), bank("bC")

        ld_x, ld_w, ld_row = sem("ld_x"), sem("ld_w"), sem("ld_row")
        init_p, xb_ok = sem("init_p"), sem("xb_ok")
        st_bn, st_mv, st_sd, st_rs = sem("st_bn"), sem("st_mv"), sem("st_sd"), sem("st_rs")
        (xn_ok, xnT_ps, xnT_ok, qk_ps, qk_ok, split, scr_ok, stk_ok, mT_ps, negm_ok, msplit, mrow_ok,
         h_ps, h_ok, v_ps, v_ok, srt_ok, gex_ok, gch, f_ps, y_ok, s_ps, mx_ok, st_ps, p_ok, pv_ok,
         o_ok, ot_ps, rd_ok, on_ok, oT_ps, oT_ok, w_ps, x1_ok, bn1, gr_ok) = [
            sem(n) for n in (
                "xn_ok", "xnT_ps", "xnT_ok", "qk_ps", "qk_ok", "split", "scr_ok", "stk_ok", "mT_ps",
                "negm_ok", "msplit", "mrow_ok", "h_ps", "h_ok", "v_ps", "v_ok", "srt_ok", "gex_ok", "gch",
                "f_ps", "y_ok", "s_ps", "mx_ok", "st_ps", "p_ok", "pv_ok", "o_ok", "ot_ps", "rd_ok",
                "on_ok", "oT_ps", "oT_ok", "w_ps", "x1_ok", "bn1", "gr_ok")]
        NLOAD = 12
        NSTK = 2 * len(Q_PART)
        NMR = NPART
        NGC = 8

        block = ctx.enter_context(nc.Block())

        def steps(body):
            def run(eng):
                for i in range(-3, 1):
                    body(eng, i, i % 2)
                with eng.Fori(1, NB - 4, 2) as i:
                    body(eng, i, 1, full=True)
                    body(eng, i + 1, 0, full=True)
                for i in range(NB - 3, NB + 1):
                    body(eng, i, i % 2)
            return run

        def has(i, off, full):
            return full or 0 <= i + off < NB

        def sync_body(eng, i, par, full=False):
            if has(i, 0, full):
                reached(eng, msplit, i, 3, 3)
                for p in range(NPART):
                    eng.dma_start(q_st[par][ROWS + p:ROWS + p + 1, :, :].rearrange("o h n -> o (h n)"),
                                  m_parts[:, p, :]).then_inc(mrow_ok, 16)
            if has(i, 2, full):
                reached(eng, split, i + 2, 3, 3)
                q_out = a["q_scr"][bass.ds(i + 2, 1)].rearrange("o r h n -> (o r) h n")
                k_out = a["k_scr"][bass.ds(i + 2, 1)].rearrange("o r h n -> (o r) h n")
                for c, (pq, pk) in enumerate(zip(Q_PART, K_PART)):
                    r = slice(c * HD, (c + 1) * HD)
                    eng.dma_start(q_out[r].rearrange("d h n -> h d n"),
                                  qk_parts[:, pq, 0:T]).then_inc(scr_ok, 16)
                    eng.dma_start(k_out[r].rearrange("d h n -> h d n"),
                                  qk_parts[0:NKV * HD, pk, T:2 * T]).then_inc(scr_ok, 16)
                reached(eng, scr_ok, i + 2, 16 * NSTK, 16 * NSTK)
                reached(eng, st_ps, i, NH, NH)
                if isinstance(i, int) and i + 2 < 2:
                    eng.wait_ge(init_p, 2)
                eng.dma_start(q_st[par][0:ROWS, :, :], q_out).then_inc(stk_ok, 16)
                eng.dma_start(k_st[par][0:ROWS, :, :], k_out).then_inc(stk_ok, 16)

        @block.sync
        def _(eng):
            for c in range(4):
                n = NT // 4
                eng.dma_start(x_sb[:, c * n:(c + 1) * n, :], a["x"][:, c * n:(c + 1) * n, :]).then_inc(ld_x, 16)
            eng.dma_start(ident[:, :], a["ident"]).then_inc(ld_w, 16)
            eng.dma_start(wq[:, :], w["Wq"]).then_inc(ld_w, 16)
            for r in range(4):
                eng.dma_start(wk4[:, r, :], w["Wk"]).then_inc(ld_w, 16)
            eng.dma_start(wv[:, :], w["Wv"]).then_inc(ld_w, 16)
            eng.dma_start(w1[:, :], w["ew1"]).then_inc(ld_w, 16)
            eng.dma_start(w2[:, :, :], w["ew2"].rearrange("(k p) n -> p k n", p=P)).then_inc(ld_w, 16)
            eng.dma_start(wg[:, :], w["Wg"]).then_inc(ld_w, 16)
            eng.dma_start(wo[:, :], w["Wo"]).then_inc(ld_w, 16)
            eng.dma_start(bq_c[:, :], w["bq"].rearrange("(p o) -> p o", o=1)).then_inc(ld_w, 16)
            for dst, src in t["loads"]:
                eng.dma_start(dst, src).then_inc(done["ld1"], 16)
            steps(sync_body)(eng)

        def pe_body(eng, i, par, full=False):
            od = 1 - par
            mm = eng.matmul

            def scores(n):
                if not has(i, 1, full):
                    return
                q, pair = n // (NH // 2), n % (NH // 2)
                if n == 0:
                    reached(eng, stk_ok, i + 1, 32, 32)
                reached(eng, mx_ok, i + 1, NH, n - 1)
                for j in range(2):
                    last = mm(s_bank[n % 2][:, j * T:(j + 1) * T],
                              q_st[od][0:ROWS, 2 * pair + j, q * P:(q + 1) * P],
                              k_st[od][0:ROWS, 2 * pair // G, :], start=True, stop=True)
                last.then_inc(s_ps, 1)

            def pv(b_par, b, grp):
                kt = grp % 2
                reached(eng, p_ok, b, NH, 4 * grp + 4)
                if grp == 0:
                    reached(eng, o_ok, b, 2, 0)
                    reached(eng, v_ok, b, 1, 1)
                if grp == 2:
                    reached(eng, o_ok, b, 2, 1)
                for kv in range(NKV):
                    last = mm(pv_bank[kv * VW:(kv + 1) * VW, :], v_sb[b_par][:, kt, kv, :],
                              pt[:, (4 * grp + kv) % 8, :], start=(kt == 0), stop=(kt == 1))
                last.then_inc(pv_ok, 1)

            def o_transposes(b, gp, dst):
                reached(eng, o_ok, b, 2, gp + 1)
                for q in range(TPB):
                    for g in range(2):
                        c = q * 2 + g
                        last = eng.transpose(dst[:, c * P:(c + 1) * P],
                                             o_sb[:, gp, g * T + q * P:g * T + (q + 1) * P], ident[:, :])
                last.then_inc(ot_ps, 1)

            def ffn_in(half):
                if not has(i, 1, full):
                    return
                if half == 0:
                    reached(eng, xnT_ok, i + 1, 1, 1)
                    reached(eng, on_ok, i - 1, 2, 1)
                    reached(eng, y_ok, i, 1, 1)
                else:
                    reached(eng, h_ok, i + 1, 2, 1)
                for j in range(2):
                    c = 2 * half + j
                    last = mm(bB[:, j * T:(j + 1) * T], w1[:, c * P:(c + 1) * P], xnT[od][:, :],
                              start=True, stop=True)
                last.then_inc(h_ps, 1)

            def ffn_out():
                if not has(i, 1, full):
                    return
                reached(eng, h_ok, i + 1, 2, 2)
                for q in range(TPB):
                    for c in range(KC):
                        last = mm(bB[:, q * P:(q + 1) * P], hT[:, c, q * P:(q + 1) * P], w2[:, c, :],
                                  start=(c == 0), stop=(c == KC - 1))
                last.then_inc(f_ps, 1)

            def tail_heads():
                if not has(i, -1, full):
                    return
                reached(eng, qk_ok, i + 2 if has(i, 2, full) else NB - 1, 1, 1)
                o_transposes(i - 1, 1, bA)

            def tail_back():
                if not has(i, -1, full):
                    return
                reached(eng, on_ok, i - 1, 2, 2)
                nxt = i + 1 if has(i, 1, full) else NB - 1
                reached(eng, v_ok, nxt, 1, 1)
                reached(eng, srt_ok, nxt, 2, 2)
                if has(i, 0, full):
                    reached(eng, negm_ok, i, 1, 1)
                for q in range(TPB):
                    last = eng.transpose(bC[:, q * P:(q + 1) * P], on[:, q, :], ident[:, :])
                last.then_inc(oT_ps, 1)

            def tail_out():
                if not has(i, -1, full):
                    return
                reached(eng, oT_ok, i - 1, 1, 1)
                for q in range(TPB):
                    last = mm(bC[:, q * P:(q + 1) * P], oT[:, q * P:(q + 1) * P], wo[:, :],
                              start=True, stop=True)
                last.then_inc(w_ps, 1)

            if has(i, 0, full):
                reached(eng, mx_ok, i, NH, NH)
                reached(eng, v_ok, i, 1, 1)
                reached(eng, srt_ok, i, 2, 2)
                eng.transpose(bC[0:TPB * NH, 0:P], mx[:, :, :].rearrange("p h q -> p (h q)"),
                              ident[:, :]).then_inc(mT_ps, 1)
            if has(i, -1, full):
                pv(od, i - 1, 3)
            if has(i, 2, full):
                reached(eng, xn_ok, i + 2, 1, 1)
                reached(eng, qk_ok, i + 1, 1, 1)
                for q in range(TPB):
                    last = eng.transpose(bA[:, q * P:(q + 1) * P], xn[:, q, :], ident[:, :])
                last.then_inc(xnT_ps, 1)
            ffn_in(0)
            if has(i, 2, full):
                reached(eng, xnT_ok, i + 2, 1, 1)
                mm(bA[:, 0:T], wq[:, :], xnT[par][:, :], start=True, stop=True)
                mm(bA[:, T:2 * T], wk4[:, :, :].rearrange("p r n -> p (r n)"), xnT[par][:, :],
                   start=True, stop=True).then_inc(qk_ps, 1)
            scores(0)
            scores(1)
            if has(i, 1, full):
                reached(eng, negm_ok, i, 1, 1)
                for q in range(TPB):
                    mm(bC[:, q * 32:(q + 1) * 32], xnT[od][:, q * P:(q + 1) * P], wv[:, :],
                       start=True, stop=True)
                    last = mm(bC[:, 128 + q * NE:128 + (q + 1) * NE], xnT[od][:, q * P:(q + 1) * P],
                              wg[:, :], start=True, stop=True)
                last.then_inc(v_ps, 1)
            ffn_in(1)
            scores(2)
            scores(3)
            ffn_out()
            nxt_s = 4
            for n in range(NH):
                if has(i, 0, full):
                    gp, kt, kv = n // 8, n // 4 % 2, n % 4
                    if n == 0:
                        reached(eng, mrow_ok, i, 16 * NMR, 16 * NMR)
                    reached(eng, p_ok, i, NH, n - 1)
                    h0 = kv * G + 2 * gp
                    mm(st_bank[n % 2][:, :], k_st[par][:, kv, kt * P:(kt + 1) * P],
                       q_st[par][:, h0:h0 + 2, :].rearrange("r h n -> r (h n)"),
                       start=True, stop=True).then_inc(st_ps, 1)
                if n % 4 != 3:
                    scores(nxt_s)
                    nxt_s += 1
                if n in (1, 4, 7):
                    {1: tail_heads, 4: tail_back, 7: tail_out}[n]()
                if has(i, 0, full):
                    if n == 5:
                        pv(par, i, 0)
                    if n == 9:
                        pv(par, i, 1)
                    if n == 13:
                        nxt = i + 1 if has(i, 1, full) else NB - 1
                        reached(eng, y_ok, nxt, 1, 1)
                        o_transposes(i, 0, bB)
                        pv(par, i, 2)

        @block.tensor
        def _(eng):
            eng.wait_ge(ld_w, 16 * NLOAD)
            steps(pe_body)(eng)

        def act_body(eng, i, par, full=False):
            od = 1 - par
            if has(i, -1, full):
                reached(eng, pv_ok, i - 1, 4, 4)
                eng.activation(o_sb[:, 1, :], pv_bank[:, :], ACT.Copy).then_inc(o_ok, 1)
            if has(i, 2, full):
                reached(eng, xnT_ps, i + 2, 1, 1)
                reached(eng, f_ps, i, 1, 1)
                reached(eng, v_ps, i, 1, 1)
                eng.activation(xnT[par][:, :], bA[:, 0:T], ACT.Copy).then_inc(xnT_ok, 1)
            if has(i, 0, full):
                reached(eng, mT_ps, i, 1, 1)
                reached(eng, msplit, i - 1, 3, 3)
                reached(eng, mrow_ok, i - 1, 16 * NMR, 16 * NMR)
                eng.activation(m_parts[:, 0, :], bC[0:TPB * NH, 0:P], ACT.Copy, scale=-1.0)
                eng.activation(negm[:, :], bC[0:TPB * NH, 0:P], ACT.Copy, scale=-1.0).then_inc(negm_ok, 1)

            def relu(half):
                if has(i, 1, full):
                    reached(eng, h_ps, i + 1, 2, half + 1)
                    reached(eng, f_ps, i, 1, 1)
                    eng.activation(hT[:, 2 * half:2 * half + 2, :],
                                   bB[:, :].rearrange("p (c n) -> p c n", c=2), ACT.Relu).then_inc(h_ok, 1)

            relu(0)
            if has(i, 2, full):
                reached(eng, qk_ps, i + 2, 1, 1)
                reached(eng, split, i + 1, 3, 3)
                reached(eng, scr_ok, i + 1, 16 * NSTK, 16 * NSTK)
                for half, bias in ((0, bq_c), (1, bk_c)):
                    c = slice(half * T, (half + 1) * T)
                    eng.activation(qk[:, c], bA[:, c], ACT.Identity, bias=bias[:, 0:1])
                    last = eng.activation(qk_parts[:, 0, c], bA[:, c], ACT.Identity, bias=bias[:, 0:1])
                last.then_inc(qk_ok, 1)
            relu(1)
            if has(i, 1, full):
                reached(eng, gch, i + 1, NGC, 1)
                reached(eng, gch, i, NGC, NGC)
                eng.activation(gex[:, :, :], gd[:, :, :], ACT.Exp).then_inc(gex_ok, 1)
            for n in range(NH):
                if has(i, 0, full):
                    reached(eng, st_ps, i, NH, n + 1)
                    if n % 4 == 0:
                        reached(eng, pv_ok, i, 4, n // 4 - 1)
                    eng.activation(pt[:, n % 8, :], st_bank[n % 2][:, :], ACT.Exp,
                                   scale=HD ** -0.5).then_inc(p_ok, 1)
                    if n == 10:
                        reached(eng, pv_ok, i, 4, 2)
                        reached(eng, ot_ps, i - 1, 2, 1)
                        eng.activation(o_sb[:, 0, :], pv_bank[:, :], ACT.Copy).then_inc(o_ok, 1)

        @block.scalar
        def _(eng):
            eng.dma_start(bo_bc[:, :], a["bo_bc"]).then_inc(ld_row, 16)
            eng.dma_start(bv_bc[:, :], a["bv_bc"]).then_inc(ld_row, 16)
            for r in range(4):
                n = NKV * HD
                eng.dma_start(bk_c[r * n:(r + 1) * n, :], w["bk"].rearrange("(p o) -> p o", o=1)).then_inc(ld_row, 16)
            eng.wait_ge(st_mv, 2)
            eng.activation(std[:, :], t["veps"][:, :], ACT.Sqrt).then_inc(st_sd, 1)
            eng.wait_ge(ld_w, 16 * NLOAD)
            eng.wait_ge(ld_row, 16 * 6)
            steps(act_body)(eng)

        def dve_body(eng, i, par, full=False):
            od = 1 - par

            def maxima(n):
                if not has(i, 1, full):
                    return
                q, pair = n // (NH // 2), n % (NH // 2)
                reached(eng, s_ps, i + 1, NH, n + 1)
                if n == 0:
                    reached(eng, mT_ps, i, 1, 1)
                eng.tensor_reduce(mx[:, 2 * pair:2 * pair + 2, q], s_bank[n % 2][:, :].rearrange("p (h k) -> p h k", h=2),
                                  AX.X, ALU.max).then_inc(mx_ok, 1)

            def heads(b, gp, src):
                reached(eng, ot_ps, b, 2, gp + 1)
                v = src[:, :].rearrange("p (q c w) -> p q c w", q=TPB, w=VW)
                r = rden[:, gp, :].rearrange("p (q c o) -> p q c o", q=TPB, o=1)
                eng.reciprocal(r, v[:, :, :, HD:HD + 1]).then_inc(rd_ok, 1)
                reached(eng, rd_ok, b, 2, gp + 1)
                half = on[:, :, gp * P // 2:(gp + 1) * P // 2]
                eng.tensor_tensor(half.rearrange("p q (c d) -> p q c d", d=HD), v[:, :, :, 0:HD],
                                  r.broadcast_to([P, TPB, NH // 2, HD]), ALU.mult).then_inc(on_ok, 1)

            maxima(0)
            maxima(1)
            if has(i, 1, full):
                reached(eng, v_ps, i + 1, 1, 1)
                reached(eng, pv_ok, i - 1, 4, 4)
                reached(eng, gch, i, NGC, 1)
                eng.tensor_tensor(v_sb[od][:, :, :, 0:HD],
                                  bC[:, 0:64].rearrange("p (q k d) -> p q k d", q=TPB, k=NKV),
                                  bv_bc[:, :].rearrange("p (o k d) -> p o k d", o=1, k=NKV)
                                  .broadcast_to([P, TPB, NKV, HD]), ALU.add).then_inc(v_ok, 1)
                for q in range(TPB):
                    eng.max(srt[:, q, :], bC[:, 128 + q * NE:128 + (q + 1) * NE]).then_inc(srt_ok, 1)
            for n in range(2, 5):
                maxima(n)
            if has(i, -1, full):
                heads(i - 1, 1, bA)
            maxima(5)
            maxima(6)
            if has(i, -1, full):
                reached(eng, oT_ps, i - 1, 1, 1)
                eng.tensor_copy(oT[:, :], bC[:, 0:T]).then_inc(oT_ok, 1)
            maxima(7)
            maxima(8)
            maxima(9)
            if has(i, -1, full):
                reached(eng, w_ps, i - 1, 1, 1)
                reached(eng, y_ok, i - 1, 1, 1)
                tile0 = (i - 1) * TPB
                eng.tensor_tensor(x1[:, bass.ds(tile0, TPB), :], xb_sb[:, bass.ds(tile0, TPB), :],
                                  bC[:, 0:T].rearrange("p (q n) -> p q n", q=TPB), ALU.add).then_inc(x1_ok, 1)
                reached(eng, x1_ok, i - 1, 1, 1)
                for q in range(TPB):
                    eng.bn_stats(t["bst1"][:, bass.ds(tile0 + q, 1), :].rearrange("p o s -> p (o s)"),
                                 x1[:, bass.ds(tile0 + q, 1), :].rearrange("p o n -> p (o n)")).then_inc(bn1, 1)
            for n in range(10, 14):
                maxima(n)
                if n in (11, 13) and has(i, 1, full):
                    src, dst, step = (gz, grz, 4) if n == 11 else (gm, grm, 6)
                    reached(eng, gch, i + 1, NGC, step)
                    if n == 13:
                        eng.tensor_scalar(gm[:, :, :], gs[:, :, :], F32_EPS, None, ALU.max).then_inc(gr_ok, 1)
                        reached(eng, gr_ok, i + 1, 3, 2)
                    eng.reciprocal(dst[:, :, :], src[:, :, :]).then_inc(gr_ok, 1)
            if has(i, 1, full):
                reached(eng, f_ps, i + 1, 1, 1)
                reached(eng, gch, i + 1, NGC, NGC)
                for q in range(TPB):
                    row = xb_sb[:, bass.ds((i + 1) * TPB + q, 1), :].rearrange("p o n -> p (o n)")
                    last = eng.scalar_tensor_tensor(row, bB[:, q * P:(q + 1) * P], gate[:, q, 0:1], row,
                                                    ALU.mult, ALU.add)
                last.then_inc(y_ok, 1)
            for n in range(14, 16):
                maxima(n)
            if has(i, 0, full):
                heads(i, 0, bB)
            if has(i, 3, full):
                reached(eng, xnT_ps, i + 2, 1, 1)
                for q in range(TPB):
                    c = (i + 3) * TPB + q
                    last = eng.tensor_scalar(xn[:, q, :], x_sb[:, bass.ds(c, 1), :].rearrange("p o n -> p (o n)"),
                                             mv[:, bass.ds(c, 1), 0:1].rearrange("p o s -> p (o s)"),
                                             rstd[:, bass.ds(c, 1)], ALU.subtract, ALU.mult)
                last.then_inc(xn_ok, 1)

        @block.vector
        def _(eng):
            for p in range(2):
                eng.memset(v_sb[p][:, :, :, :], 0.0).then_inc(done["dv"], 1)
            eng.wait_ge(done["dv"], 2)
            for p in range(2):
                eng.memset(v_sb[p][:, :, :, HD:HD + 1], 1.0).then_inc(v_init := done["dv"], 1)
            for c in range(NT):
                if c % (NT // 4) == 0:
                    eng.wait_ge(ld_x, 16 * 4)
                eng.bn_stats(bst[:, c, :], x_sb[:, c, :]).then_inc(st_bn, 1)
            eng.wait_ge(st_bn, NT)
            for c in range(NT):
                last = eng.bn_aggr(mv[:, c, :], bst[:, c, :])
            last.then_inc(st_mv, 1)
            eng.wait_ge(st_mv, 1)
            eng.tensor_scalar(t["veps"][:, :], mv[:, :, 1], LN_EPS, None, ALU.add).then_inc(st_mv, 1)
            eng.wait_ge(st_sd, 1)
            eng.reciprocal(rstd[:, :], std[:, :]).then_inc(st_rs, 1)
            eng.wait_ge(st_rs, 1)
            eng.wait_ge(done["dv"], 4)
            eng.wait_ge(ld_row, 16 * 6)
            eng.wait_ge(xb_ok, 1)
            steps(dve_body)(eng)

        def pool_body(eng, i, par, full=False):
            TT = eng.tensor_tensor
            if has(i, 0, full):
                reached(eng, negm_ok, i, 1, 1)
                TT(negm_rest[:, :], negm[:, :], m_parts[:, 0, :], ALU.subtract).then_inc(msplit, 1)
                TT(m_parts[:, 1, :], negm[:, :], m_parts[:, 0, :], ALU.subtract).then_inc(msplit, 1)
                reached(eng, msplit, i, 3, 2)
                TT(m_parts[:, 2, :], negm_rest[:, :], m_parts[:, 1, :], ALU.subtract).then_inc(msplit, 1)
            if has(i, 1, full):
                reached(eng, srt_ok, i + 1, 2, 2)
                reached(eng, gex_ok, i, 1, 1)
                TT(gd[:, :, :], srt[:, :, :], srt[:, :, 0:1].broadcast_to([P, TPB, NE]),
                   ALU.subtract).then_inc(gch, 1)
            if has(i, 2, full):
                reached(eng, qk_ok, i + 2, 1, 1)
                TT(qk_rest[:, :], qk[:, :], qk_parts[:, 0, :], ALU.subtract).then_inc(split, 1)
                TT(qk_parts[:, 1, :], qk[:, :], qk_parts[:, 0, :], ALU.subtract).then_inc(split, 1)
                reached(eng, split, i + 2, 3, 2)
                TT(qk_parts[:, 2, :], qk_rest[:, :], qk_parts[:, 1, :], ALU.subtract).then_inc(split, 1)
            if has(i, 1, full):
                b = i + 1
                reached(eng, gex_ok, b, 1, 1)
                chain = [
                    lambda: TT(g4[:, :, :], gex[:, :, 0:4], gex[:, :, 4:8], ALU.add),
                    lambda: TT(g2[:, :, :], g4[:, :, 0:2], g4[:, :, 2:4], ALU.add),
                    lambda: TT(gz[:, :, :], g2[:, :, 0:1], g2[:, :, 1:2], ALU.add),
                    lambda: TT(gp2[:, :, :], gex[:, :, 0:2], grz[:, :, :].broadcast_to([P, TPB, 2]), ALU.mult),
                    lambda: TT(gs[:, :, :], gp2[:, :, 0:1], gp2[:, :, 1:2], ALU.add),
                    lambda: TT(gq[:, :, :], gp2[:, :, :], grm[:, :, :].broadcast_to([P, TPB, 2]), ALU.mult),
                    lambda: TT(gate[:, :, :], gq[:, :, 0:1], gq[:, :, 1:2], ALU.add),
                ]
                for k, op in enumerate(chain):
                    if k in (3, 5):
                        reached(eng, gr_ok, b, 3, 1 if k == 3 else 3)
                    if k == len(chain) - 1:
                        reached(eng, y_ok, b - 1, 1, 1)
                    op().then_inc(gch, 1)
                    reached(eng, gch, b, NGC, k + 2)

        @block.gpsimd
        def _(eng):
            for p in range(2):
                eng.memset(k_st[p][:, :, :], 1.0).then_inc(init_p, 1)
            eng.wait_ge(ld_x, 16 * 4)
            eng.wait_ge(ld_row, 16 * 6)
            eng.tensor_tensor(xb_sb[:, :, :], x_sb[:, :, :],
                              bo_bc[:, :].rearrange("p (o n) -> p o n", o=1).broadcast_to([P, NT, P]),
                              ALU.add).then_inc(xb_ok, 1)
            steps(pool_body)(eng)


def layer1(nc, w, t, done, out):
    ctx = ExitStack()
    with ctx:
        def sb(name, shape, dt=F32):
            return ctx.enter_context(nc.sbuf_tensor(name, shape, dt))

        def sem(name):
            return ctx.enter_context(nc.semaphore(name))

        def bank(name):
            return ctx.enter_context(nc.psum_tensor(name, [P, GT], F32))

        NTOK = NB * T
        x1, ident, bst1 = t["x1"], t["ident"], t["bst1"]
        (win, wdt, wx, wout, w1, w2, h1, h2, w3) = (t[n] for n in
            ("win", "wdt", "wx", "wout", "f1", "f2", "fh1", "fh2", "f3"))
        mv, std, rstd = sb("mv1", [P, NT, 2]), sb("std1", [P, NT]), sb("rstd1", [P, NT])
        w3s = sb("w3s", [P, KC, P])
        nega = sb("nega", [P, CI, NS])
        wx_p = sb("wx_p", [P, CI, NPART * 32])
        sel = sb("sel", [NPART * 32, NS, P], BF16)
        xn = sb("xn_1", [P, GTT, P])
        xnT = sb("xnT_1", [P, NTOK])
        sil = sb("sil", [P, KC, GT])
        g2 = sb("gelu2", [P, KC, GT])
        g3 = sb("gelu3", [P, KC, GT])
        xc = sb("xc", [P, CI, GT])
        xs, zs, dt = sb("xs", [P, CI, NTOK]), sb("zs", [P, CI, NTOK]), sb("dt", [P, CI, GT])
        u_abs, u_pos = sb("u_abs", [P, CI, GT]), sb("u_pos", [P, CI, GT])
        e_sb, l_sb = sb("e_sb", [P, CI, GT]), sb("l_sb", [P, CI, GT])
        b_full, b_rest = sb("b_full", [NPART * 32, GT]), sb("b_rest", [NPART * 32, GT])
        b_mid = sb("b_mid", [NPART * 32, GT], BF16)
        b_parts = sb("b_parts", [NPART * 32, NTOK], BF16)
        NR = 8
        da = sb("da", [P, NR, GB, T])
        hb = sb("hb", [P, NR, GT])
        acc = sb("acc", [P, CI, GT])
        y = sb("y", [P, CI, GT])
        o = sb("o", [P, GTT, P])

        f_bank = [bank(f"f_bank{i}") for i in range(4)]
        b_bank = [bank(f"b_bank{i}") for i in range(2)]
        pA, pB = bank("pA"), bank("pB")

        (i_act, i_dve, i_pool, xn_ok, xT_ps, xT_ok, l1_ps, sil_ok, h0_ok, win_ps, z_ok, cv_ok, conv, xs_ok,
         dt_ps, u_ok, sp_ok, spd, bx_ps, bx_ok, bsp, b_ps, da_ok, scan, acc0, acc1, y_ok, l2_ps, g2_ok,
         l3_ps, g3_ok, o_ps, o_ok, out_ok, acc1_0) = [sem("b_" + n) for n in (
             "i_act", "i_dve", "i_pool", "xn_ok", "xT_ps", "xT_ok", "l1_ps", "sil_ok", "h0_ok", "win_ps",
             "z_ok", "cv_ok", "conv", "xs_ok", "dt_ps", "u_ok", "sp_ok", "spd", "bx_ps", "bx_ok", "bsp",
             "b_ps", "da_ok", "scan", "acc0", "acc1", "y_ok", "l2_ps", "g2_ok", "l3_ps", "g3_ok", "o_ps",
             "o_ok", "out_ok", "acc1_0")]
        NSP = 4

        block = ctx.enter_context(nc.Block())

        def steps(body):
            def run(eng):
                body(eng, -1)
                body(eng, 0)
                with eng.Fori(1, NG - 1) as g:
                    body(eng, g, full=True)
                body(eng, NG - 1)
                body(eng, NG)
            return run

        def has(g, off, full):
            return full or 0 <= g + off < NG

        def cols(g):
            return bass.ds(g * GT, GT)

        def sync_body(eng, g, full=False):
            if has(g, -1, full):
                reached(eng, o_ok, g - 1, 1, 1)
                eng.dma_start(out[:, bass.ds((g - 1) * GTT, GTT), :], o[:, :, :]).then_inc(out_ok, 16)

        @block.sync
        def _(eng):
            steps(sync_body)(eng)
            eng.wait_ge(out_ok, 16 * NG)

        def pe_body(eng, g, full=False):
            mm = eng.matmul
            nx, cur, prv = has(g, 1, full), has(g, 0, full), has(g, -1, full)
            state = [0]

            def b_row(keep=False):
                s = state[0]
                if not cur or s >= NS:
                    return
                state[0] += 1
                if s == 0:
                    reached(eng, bsp, g, 4, 4)
                reached(eng, scan, g, 2 * NS, 2 * (s - 1))
                mm(b_bank[s % 2][:, :], sel[:, s, :], b_parts[:, cols(g)], start=True,
                   stop=True).then_inc(b_ps, 1)

            def ffn1(c):
                if not cur:
                    return
                fa, fb = f_bank[2 * (c % 2)], f_bank[2 * (c % 2) + 1]
                if c < 2:
                    reached(eng, g3_ok, g - 1, KC, 2 * c + 2)
                    reached(eng, xT_ok, g, 1, 1)
                else:
                    reached(eng, h0_ok, g, KC, c - 1)
                mm(fa[:, :], w1[:, c * P:(c + 1) * P], xnT[:, cols(g)], start=True, stop=True)
                mm(fb[:, :], w2[:, c * P:(c + 1) * P], xnT[:, cols(g)], start=True, stop=True).then_inc(l1_ps, 1)

            def w_in(c, dst):
                if nx:
                    mm(dst[:, :], win[:, c * P:(c + 1) * P], xnT[:, cols(g + 1)], start=True,
                       stop=True).then_inc(win_ps, 1)

            def hidden(c, wt, src, ready, free, done_sem):
                if not cur:
                    return
                for k in range(KC):
                    reached(eng, ready, g, KC, k + 1)
                    if k == 0:
                        reached(eng, *free)
                    last = mm(f_bank[c][:, :], wt[:, k, c * P:(c + 1) * P], src[:, k, :],
                              start=(k == 0), stop=(k == KC - 1))
                    if k % 2:
                        b_row() if k < KC - 1 else None
                last.then_inc(done_sem, 1)
                b_row()

            if nx:
                reached(eng, xn_ok, g + 1, 1, 1)
                reached(eng, bx_ok, g, 1, 1)
                for q in range(GTT):
                    last = eng.transpose(pA[:, q * P:(q + 1) * P], xn[:, q, :], ident[:, :])
                last.then_inc(xT_ps, 1)
            b_row()
            b_row()
            ffn1(0)
            ffn1(1)
            if nx:
                reached(eng, u_ok, g, 4, 4)
                reached(eng, xT_ok, g + 1, 1, 1)
                w_in(2, pB)
                w_in(3, pA)
            ffn1(2)
            ffn1(3)
            if nx:
                reached(eng, z_ok, g + 1, 2, 1)
                w_in(0, pB)
                reached(eng, z_ok, g + 1, 2, 2)
                w_in(1, pA)
            if prv:
                if nx:
                    reached(eng, conv, g + 1, 6, 3)
                else:
                    reached(eng, u_ok, NG - 1, 4, 4)
                reached(eng, y_ok, g - 1, 2, 2)
                reached(eng, g3_ok, g - 1, KC, KC)
                for q in range(GTT):
                    r = slice(q * P, (q + 1) * P)
                    for k in range(KC):
                        mm(pB[:, r], g3[:, k, r], w3s[:, k, :], start=(k == 0), stop=False)
                    for c in range(CI):
                        last = mm(pB[:, r], y[:, c, r], wout[:, c, :], start=False, stop=(c == CI - 1))
                last.then_inc(o_ps, 1)

            def second(c):
                hidden(c, h1, sil, h0_ok, (h0_ok, g, KC, 3 if c < 2 else 4), l2_ps)

            second(0)
            if nx:
                reached(eng, xs_ok, g + 1, 2, 2)
                reached(eng, conv, g + 1, 6, 6)
                for c in range(CI):
                    last = mm(pA[0:NPART * 32, :], wx_p[:, c, :], xs[:, c, cols(g + 1)],
                              start=(c == 0), stop=(c == CI - 1))
                last.then_inc(bx_ps, 1)
            second(1)

            def step_in(c, dst, *free):
                if nx:
                    reached(eng, *free)
                    for k in range(CI):
                        last = mm(dst[:, :], wdt[:, k, c * P:(c + 1) * P], xs[:, k, cols(g + 1)],
                                  start=(k == 0), stop=(k == CI - 1))
                    last.then_inc(dt_ps, 1)
                    b_row()

            step_in(0, pA, bx_ok, g + 1, 1, 1)
            second(2)
            step_in(1, pB, o_ok, g - 1, 1, 1)
            second(3)
            for c in range(KC):
                hidden(c, h2, g2, g2_ok, (g2_ok, g, KC, c + 1), l3_ps)
            while cur and state[0] < NS:
                b_row()

        @block.tensor
        def _(eng):
            eng.wait_ge(done["ld1"], 16 * len(t["loads"]))
            eng.wait_ge(i_pool, 5)
            eng.wait_ge(i_dve, 3)
            steps(pe_body)(eng)

        def act_body(eng, g, full=False):
            nx, cur, prv = has(g, 1, full), has(g, 0, full), has(g, -1, full)
            act = eng.activation
            if nx:
                reached(eng, xT_ps, g + 1, 1, 1)
                settled(eng, i_pool, 5)
                act(xnT[:, cols(g + 1)], pA[:, :], ACT.Copy).then_inc(xT_ok, 1)

            def ffn_silu(c):
                if cur:
                    reached(eng, l1_ps, g, KC, c + 1)
                    reached(eng, l2_ps, g - 1, KC, KC)
                    act(sil[:, c, :], f_bank[2 * (c % 2)][:, :], ACT.Silu,
                        scale=t["f1s"][:, c:c + 1]).then_inc(sil_ok, 1)

            ffn_silu(0)
            ffn_silu(1)
            if nx:
                for c, src in ((0, pB), (1, pA)):
                    reached(eng, win_ps, g + 1, 4, c + 1)
                    settled(eng, i_pool, 5)
                    act(zs[:, c, cols(g + 1)], src[:, :], ACT.Silu).then_inc(z_ok, 1)
            ffn_silu(2)
            ffn_silu(3)
            if nx:
                for c, src in ((0, pB), (1, pA)):
                    reached(eng, win_ps, g + 1, 4, c + 3)
                    reached(eng, xs_ok, g, 2, 2)
                    act(xc[:, c, :], src[:, :], ACT.Identity, bias=t["cb"][:, c:c + 1],
                        scale=t["cw"][:, c, TAPS - 1:TAPS]).then_inc(cv_ok, 1)
                for c in range(CI):
                    reached(eng, conv, g + 1, 6, 3 * c + 3)
                    settled(eng, i_pool, 5)
                    act(xs[:, c, cols(g + 1)], xc[:, c, :], ACT.Silu).then_inc(xs_ok, 1)

            def decay(s):
                if not cur:
                    return
                if s == 0:
                    reached(eng, spd, g, NSP, NSP)
                for c in range(CI):
                    n = CI * s + c
                    reached(eng, scan, g, 2 * NS, n + 1 - NR)
                    act(da[:, n % NR, :, 1:T],
                        dt[:, c, :].rearrange("p (b n) -> p b n", b=GB)[:, :, 1:T],
                        ACT.Exp, scale=nega[:, c, s:s + 1]).then_inc(da_ok, 1)

            for s in range(9):
                decay(s)
            if nx:
                reached(eng, bx_ps, g + 1, 1, 1)
                reached(eng, bsp, g, 4, 4)
                settled(eng, i_pool, 5)
                act(b_parts[:, cols(g + 1)], pA[0:NPART * 32, :], ACT.Copy)
                act(b_full[:, :], pA[0:NPART * 32, :], ACT.Copy).then_inc(bx_ok, 1)
                for c, src in ((0, pA), (1, pB)):
                    reached(eng, dt_ps, g + 1, 2, c + 1)
                    reached(eng, spd, g, NSP, NSP)
                    act(u_abs[:, c, :], src[:, :], ACT.Abs, bias=t["bdt"][:, c:c + 1]).then_inc(u_ok, 1)
                    act(u_pos[:, c, :], src[:, :], ACT.Relu, bias=t["bdt"][:, c:c + 1]).then_inc(u_ok, 1)
            if cur:
                for c in range(KC):
                    reached(eng, l2_ps, g, KC, c + 1)
                    reached(eng, l3_ps, g - 1, KC, KC)
                    act(g2[:, c, :], f_bank[c][:, :], ACT.Gelu, scale=t["h1s"][:, c:c + 1]).then_inc(g2_ok, 1)
            for s in range(9, NS):
                decay(s)
            if nx:
                reached(eng, u_ok, g + 1, 4, 4)
                act(e_sb[:, :, :], u_abs[:, :, :], ACT.Exp, scale=-1.0).then_inc(sp_ok, 1)
                reached(eng, spd, g + 1, NSP, 1)
                act(l_sb[:, :, :], u_abs[:, :, :], ACT.Ln).then_inc(sp_ok, 1)
            if cur:
                for c in range(KC):
                    reached(eng, l3_ps, g, KC, c + 1)
                    reached(eng, o_ps, g - 1, 1, 1)
                    act(g3[:, c, :], f_bank[c][:, :], ACT.Gelu, scale=t["h2s"][:, c:c + 1]).then_inc(g3_ok, 1)

        @block.scalar
        def _(eng):
            eng.wait_ge(done["ld1"], 16 * len(t["loads"]))
            eng.wait_ge(i_dve, 2)
            eng.activation(std[:, :], t["veps"][:, :], ACT.Sqrt).then_inc(i_act, 1)
            eng.activation(nega[:, :, :], t["alog"][:, :, :], ACT.Exp).then_inc(i_act, 1)
            eng.wait_ge(i_dve, 5)
            eng.wait_ge(i_pool, 5)
            steps(act_body)(eng)

        def dve_body(eng, g, full=False):
            nx, cur, prv = has(g, 1, full), has(g, 0, full), has(g, -1, full)
            STT = eng.scalar_tensor_tensor

            def ffn_mul(c):
                if cur:
                    reached(eng, sil_ok, g, KC, c + 1)
                    STT(sil[:, c, :], f_bank[2 * (c % 2) + 1][:, :], t["f2s"][:, c:c + 1], sil[:, c, :],
                        ALU.mult, ALU.mult).then_inc(h0_ok, 1)

            if nx:
                normalise(eng, g + 1)
            for c in range(KC):
                ffn_mul(c)
            if nx:
                for c, src in ((0, pB), (1, pA)):
                    acc_v = xc[:, c, :].rearrange("p (b n) -> p b n", b=GB)
                    src_v = src[:, :].rearrange("p (b n) -> p b n", b=GB)
                    reached(eng, cv_ok, g + 1, 2, c + 1)
                    for k in range(1, TAPS):
                        if k > 1:
                            reached(eng, conv, g + 1, 6, 3 * c + k - 1)
                        STT(acc_v[:, :, k:T], src_v[:, :, 0:T - k], t["cw"][:, c, TAPS - 1 - k:TAPS - k],
                            acc_v[:, :, k:T], ALU.mult, ALU.add).then_inc(conv, 1)
            for s in range(NS):
                if cur:
                    reached(eng, b_ps, g, NS, s + 1)
                    for c in range(CI):
                        n = CI * s + c
                        reached(eng, da_ok, g, 2 * NS, n + 1)
                        if c == 1:
                            reached(eng, acc1, g, NS - 1, s - NR // CI)
                        eng.tensor_tensor_scan(hb[:, n % NR, :],
                                               da[:, n % NR, :, :].rearrange("p b n -> p (b n)"),
                                               b_bank[s % 2][:, :], 0.0, ALU.mult, ALU.add).then_inc(scan, 1)
                    if s == 0:
                        reached(eng, scan, g, 2 * NS, 2)
                        for c in range(CI):
                            reached(eng, y_ok, g - 1, 2, c + 1)
                            STT(acc[:, c, :], xs[:, c, cols(g)], t["D"][:, c:c + 1], hb[:, c, :],
                                ALU.mult, ALU.add).then_inc((acc0, acc1_0)[c], 1)
                    else:
                        reached(eng, scan, g, 2 * NS, 2 * s + 1)
                        reached(eng, acc0, g, NS, s)
                        eng.tensor_tensor(acc[:, 0, :], acc[:, 0, :], hb[:, CI * s % NR, :],
                                          ALU.add).then_inc(acc0, 1)
                if s == 3 and prv:
                    reached(eng, o_ps, g - 1, 1, 1)
                    reached(eng, out_ok, g - 2, 16, 16)
                    eng.tensor_tensor(o[:, :, :], x1[:, bass.ds((g - 1) * GTT, GTT), :],
                                      pB[:, :].rearrange("p (q n) -> p q n", q=GTT), ALU.add).then_inc(o_ok, 1)
            if nx:
                mid, top = slice(32, 64), slice(64, 96)
                reached(eng, bsp, g + 1, 4, 2)
                eng.tensor_copy(b_parts[mid, cols(g + 1)], b_mid[mid, :]).then_inc(bsp, 1)
                eng.tensor_tensor(b_parts[top, cols(g + 1)], b_rest[top, :], b_mid[top, :],
                                  ALU.subtract).then_inc(bsp, 1)
            if nx:
                reached(eng, sp_ok, g + 1, 2, 1)
                eng.tensor_scalar(u_abs[:, :, :], e_sb[:, :, :], 1.0, None, ALU.add).then_inc(spd, 1)
                reached(eng, spd, g + 1, NSP, 1)
                STT(e_sb[:, :, :], u_abs[:, :, :], -1.0, e_sb[:, :, :], ALU.add, ALU.subtract).then_inc(spd, 1)
                reached(eng, spd, g + 1, NSP, 2)
                eng.tensor_tensor(e_sb[:, :, :], u_pos[:, :, :], e_sb[:, :, :], ALU.subtract).then_inc(spd, 1)
                reached(eng, spd, g + 1, NSP, 3)
                reached(eng, sp_ok, g + 1, 2, 2)
                eng.tensor_tensor(dt[:, :, :], e_sb[:, :, :], l_sb[:, :, :], ALU.add).then_inc(spd, 1)
            if cur:
                for c in range(CI):
                    reached(eng, acc0 if c == 0 else acc1, g, NS - c, NS - c)
                    reached(eng, o_ps, g - 1, 1, 1)
                    eng.tensor_tensor(y[:, c, :], acc[:, c, :], zs[:, c, cols(g)], ALU.mult).then_inc(y_ok, 1)

        def normalise(eng, g):
            reached(eng, xT_ps, g - 1, 1, 1)
            for q in range(GTT):
                c = g * GTT + q
                last = eng.tensor_scalar(xn[:, q, :], x1[:, bass.ds(c, 1), :].rearrange("p o n -> p (o n)"),
                                         mv[:, bass.ds(c, 1), 0:1].rearrange("p o s -> p (o s)"),
                                         rstd[:, bass.ds(c, 1)], ALU.subtract, ALU.mult)
            last.then_inc(xn_ok, 1)

        @block.vector
        def _(eng):
            for c in range(NT):
                last = eng.bn_aggr(mv[:, c, :], bst1[:, c, :])
            last.then_inc(i_dve, 1)
            eng.wait_ge(i_dve, 1)
            eng.tensor_scalar(t["veps"][:, :], mv[:, :, 1], LN_EPS, None, ALU.add).then_inc(i_dve, 1)
            eng.memset(da[:, :, :, 0:1], 0.0)
            eng.wait_ge(done["ld1"], 16 * len(t["loads"]))
            eng.tensor_tensor(w3s[:, :, :], w3[:, :, :],
                              t["w3s_bc"][:, :].rearrange("p (o n) -> p o n", o=1).broadcast_to([P, KC, P]),
                              ALU.mult).then_inc(i_dve, 1)
            eng.wait_ge(i_act, 1)
            eng.reciprocal(rstd[:, :], std[:, :]).then_inc(i_dve, 1)
            eng.wait_ge(i_act, 2)
            eng.tensor_scalar(nega[:, :, :], nega[:, :, :], -1.0, None, ALU.mult).then_inc(i_dve, 1)
            eng.wait_ge(i_dve, 5)
            steps(dve_body)(eng)

        def pool_body(eng, g, full=False):
            TT = eng.tensor_tensor
            if has(g, 0, full):
                for s in range(1, NS):
                    reached(eng, scan, g, 2 * NS, 2 * s + 2)
                    if s == 1:
                        reached(eng, acc1_0, g, 1, 1)
                    else:
                        reached(eng, acc1, g, NS - 1, s - 1)
                    TT(acc[:, 1, :], acc[:, 1, :], hb[:, (CI * s + 1) % NR, :], ALU.add).then_inc(acc1, 1)
                    if s == 10:
                        parts(eng, g + 1, has(g, 1, full))
            else:
                parts(eng, g + 1, has(g, 1, full))

        def parts(eng, g, on):
            if not on:
                return
            TT = eng.tensor_tensor
            reached(eng, bx_ok, g, 1, 1)
            settled(eng, i_dve, 1)
            TT(b_rest[:, :], b_full[:, :], b_parts[:, cols(g)], ALU.subtract).then_inc(bsp, 1)
            TT(b_mid[:, :], b_full[:, :], b_parts[:, cols(g)], ALU.subtract).then_inc(bsp, 1)

        @block.gpsimd
        def _(eng):
            eng.wait_ge(done["ld1"], 16 * len(t["loads"]))
            eng.memset(wx_p[:, :, :], 0.0).then_inc(i_pool, 1)
            eng.wait_ge(i_pool, 1)
            for p in range(NPART):
                eng.tensor_copy(wx_p[:, :, 32 * p:32 * p + NS], wx[:, :, :]).then_inc(i_pool, 1)
            eng.tensor_copy(sel[:, :, :], t["pick"][:, :].rearrange("p (s o) -> p s o", o=1)
                            .broadcast_to([NPART * 32, NS, P])).then_inc(i_pool, 1)
            steps(pool_body)(eng)


def program(nc, w, scr, out):
    x = w["x"].rearrange("b (q p) d -> p (b q) d", p=P)
    out = out.rearrange("b (q p) d -> p (b q) d", p=P)
    ctx = ExitStack()
    with ctx:
        def sb(name, shape, dt=F32):
            return ctx.enter_context(nc.sbuf_tensor(name, shape, dt))

        t = dict(ident=sb("ident", [P, P]), x1=sb("x1", [P, NT, P]), veps=sb("veps", [P, NT]),
                 bst1=sb("bst1", [P, NT, 6]))
        loads = []

        def load(name, shape, src):
            t[name] = sb("ld_" + name, shape)
            loads.append((t[name][tuple(slice(None) for _ in shape)], src))

        chunks = "(k p) n -> p k n"
        load("win", [P, 2 * DI], w["W_in"])
        load("wdt", [P, CI, DI], w["W_dt"].rearrange(chunks, p=P))
        load("wx", [P, CI, NS], w["W_x"].rearrange(chunks, p=P))
        load("wout", [P, CI, P], w["W_out"].rearrange(chunks, p=P))
        load("cw", [P, CI, TAPS], w["conv_w"].rearrange("(k p) o n -> p k (o n)", p=P))
        load("cb", [P, CI], w["conv_b"])
        load("alog", [P, CI, NS], w["A_log"].rearrange(chunks, p=P))
        load("D", [P, CI], w["D"])
        load("bdt", [P, CI], w["b_dt"])
        load("f1", [P, DFF], w["w1_t"])
        load("f2", [P, DFF], w["w2_t"])
        load("fh1", [P, KC, DFF], w["h1_t"].rearrange(chunks, p=P))
        load("fh2", [P, KC, DFF], w["h2_t"].rearrange(chunks, p=P))
        load("f3", [P, KC, P], w["w3_t"].rearrange(chunks, p=P))
        for n in ("w1", "w2", "h1", "h2"):
            load({"w1": "f1s", "w2": "f2s", "h1": "h1s", "h2": "h2s"}[n], [P, KC], w[n + "_s"])
        load("w3s_bc", [P, P], w["w3_s"].partition_broadcast(P))
        load("pick", [NPART * 32, NS], w["pick"])
        t["loads"] = loads
        done = {n: ctx.enter_context(nc.semaphore(n)) for n in ("ld1", "dv")}
        a = dict(x=x, q_scr=scr["q"], k_scr=scr["k"], ident=w["ident"],
                 bo_bc=w["bo"].partition_broadcast(P), bv_bc=w["bv"].partition_broadcast(P))
        layer0(nc, a, w, t, done)
        layer1(nc, w, t, done, out)


def kernel(**inputs):
    import numpy as _np
    import concourse.bacc as _bacc
    from concourse import mybir as _mybir
    from concourse.bass_utils import run_bass_kernel_spmd as _run

    nc = _bacc.Bacc("TRN2", target_bir_lowering=False, num_devices=1)
    host = {}
    for name, v in inputs.items():
        short = name.split("_", 2)[2]
        v = _np.asarray(v)
        if name.startswith("L1_ffn") and v.ndim == 2:
            short, v = short[:3] + "t", v.T
        elif v.ndim == 1 and v.size > P:
            v = v.reshape(-1, P).T
        elif name in ("L0_ffn_w1", "L0_ffn_w2"):
            short = "e" + short
        host[short] = _np.ascontiguousarray(v)
    host["ident"] = _np.eye(P, dtype=_np.float32)
    host["pick"] = _np.tile(_np.eye(32, NS, dtype=_np.float32), (NPART, 1))
    arrays, w = {}, {}
    for n, v in host.items():
        arrays[f"in_{n}"] = v
        w[n] = nc.dram_tensor(f"in_{n}", v.shape, _mybir.dt.from_np(v.dtype), kind="ExternalInput").ap()
    scr = {n: nc.dram_tensor(f"{n}_scr", (NB, ROWS, h, T), _mybir.dt.bfloat16, kind="Internal").ap()
           for n, h in (("q", NH), ("k", NKV))}
    out = nc.dram_tensor("out", (NB, T, P), _mybir.dt.float32, kind="ExternalOutput").ap()
    program(nc, w, scr, out)
    r = _run(nc, [arrays], core_ids=[0])
    return r.results[0]["out"]
```

```python
from contextlib import ExitStack

import numpy as np

import concourse.bass as bass
from concourse import mybir

F32, BF16 = mybir.dt.float32, mybir.dt.bfloat16
ALU, ACT, AX = mybir.AluOpType, mybir.ActivationFunctionType, mybir.AxisListType

P = 128
NB, T = 8, 256
NT = NB * T // P
TPB = T // P
NH, NKV, HD = 16, 4, 8
G = NH // NKV
NE = 8
DFF = 512
KC = DFF // P
DI = 256
CI = DI // P
NS = 16
TAPS = 4
GT = 512
NG = NB * T // GT
GB = GT // T
GTT = GT // P
LN_EPS = 1e-5
F32_EPS = float(np.finfo(np.float32).eps)
Q_PART = [0, 0, 0, 1, 1, 2]
K_PART = [0, 1, 2, 0, 1, 0]
NPART = 3
ROWS = HD * len(Q_PART)
MROWS = ROWS + NPART
VW = 32


def reached(eng, sem, b, per, k):
    v = b * per + k
    if isinstance(v, int) and v <= 0:
        return
    eng.wait_ge(sem, v)


def settled(eng, sem, v):
    eng.wait_ge(sem, v)


def layer0(nc, sb, sem, banks, a, w, t, done):
    x_sb, xb_sb = sb("x_sb", [P, NT, P]), sb("xb_sb", [P, NT, P])
    bo_bc, bv_bc = sb("bo_bc", [P, P]), sb("bv_bc", [P, NKV * HD])
    wq, wk4, wv = sb("wq", [P, P]), sb("wk4", [P, 4, NKV * HD]), sb("wv", [P, NKV * HD])
    wo, wg = sb("wo", [P, P]), sb("wg", [P, NE])
    w1, w2 = sb("w1", [P, DFF]), sb("w2", [P, KC, P])
    bq_c, bk_c = sb("bq_c", [P, 1]), sb("bk_c", [P, 1])
    bst, mv = sb("bst", [P, NT, 6]), sb("mv", [P, NT, 2])
    std, rstd = sb("std", [P, NT]), sb("rstd", [P, NT])
    xn = sb("xn", [P, TPB, P])
    xnT = [sb(f"xnT_{p}", [P, T]) for p in range(2)]
    qk = sb("qk", [P, 2 * T])
    qk_rest = sb("qk_rest", [P, 2 * T])
    qk_parts = sb("qk_parts", [P, NPART, 2 * T], BF16)
    q_st = [sb(f"q_st{p}", [MROWS, NH, T], BF16) for p in range(2)]
    k_st = [sb(f"k_st{p}", [MROWS, NKV, T], BF16) for p in range(2)]
    v_sb = [sb(f"v_sb{p}", [P, TPB, NKV, VW]) for p in range(2)]
    mx = sb("mx", [P, NH, TPB])
    negm, negm_rest = sb("negm", [TPB * NH, P]), sb("negm_rest", [TPB * NH, P])
    m_parts = sb("m_parts", [TPB * NH, NPART, P], BF16)
    pt = sb("pt", [P, 8, 512])
    o_sb = sb("o_sb", [P, 2, 512])
    on = sb("on", [P, TPB, P])
    rden = sb("rden", [P, 2, 16])
    oT = sb("oT", [P, T])
    hT = sb("hT", [P, KC, T])
    srt, gex = sb("srt", [P, TPB, NE]), sb("gex", [P, TPB, NE])
    gd, g4, g2 = sb("gd", [P, TPB, NE]), sb("g4", [P, TPB, 4]), sb("g2", [P, TPB, 2])
    gz, gp2, gs = sb("gz", [P, TPB, 1]), sb("gp2", [P, TPB, 2]), sb("gs", [P, TPB, 1])
    grz, grm = sb("grz", [P, TPB, 1]), sb("grm", [P, TPB, 1])
    gm, gq, gate = sb("gm", [P, TPB, 1]), sb("gq", [P, TPB, 2]), sb("gate", [P, TPB, 1])
    ident, x1 = t["ident"], t["x1"]

    s_bank, st_bank = banks[0:2], banks[2:4]
    pv_bank = banks[4]
    bA, bB, bC = banks[5:8]

    ld_x, ld_w, ld_row = sem("ld_x"), sem("ld_w"), sem("ld_row")
    init_p, xb_ok = sem("init_p"), sem("xb_ok")
    st_bn, st_mv, st_sd, st_rs = sem("st_bn"), sem("st_mv"), sem("st_sd"), sem("st_rs")
    (xn_ok, xnT_ps, xnT_ok, qk_ps, qk_ok, split, scr_ok, stk_ok, mT_ps, negm_ok, msplit, mrow_ok,
     h_ps, h_ok, v_ps, v_ok, srt_ok, gex_ok, gch, f_ps, y_ok, s_ps, mx_ok, st_ps, p_ok, pv_ok,
     o_ok, ot_ps, rd_ok, on_ok, oT_ps, oT_ok, w_ps, x1_ok, gr_ok) = [
        sem(n) for n in (
            "xn_ok", "xnT_ps", "xnT_ok", "qk_ps", "qk_ok", "split", "scr_ok", "stk_ok", "mT_ps",
            "negm_ok", "msplit", "mrow_ok", "h_ps", "h_ok", "v_ps", "v_ok", "srt_ok", "gex_ok", "gch",
            "f_ps", "y_ok", "s_ps", "mx_ok", "st_ps", "p_ok", "pv_ok", "o_ok", "ot_ps", "rd_ok",
            "on_ok", "oT_ps", "oT_ok", "w_ps", "x1_ok", "gr_ok")]
    NLOAD = 12
    NSTK = 2 * len(Q_PART)
    NMR = NPART
    NGC = 8

    def steps(body):
        def run(eng):
            for i in range(-3, 1):
                body(eng, i, i % 2)
            with eng.Fori(1, NB - 4, 2) as i:
                body(eng, i, 1, full=True)
                body(eng, i + 1, 0, full=True)
            for i in range(NB - 3, NB):
                body(eng, i, i % 2)
        return run

    def has(i, off, full):
        return full or 0 <= i + off < NB

    def sync_body(eng, i, par, full=False):
        if has(i, 0, full):
            reached(eng, msplit, i, 3, 3)
            for p in range(NPART):
                eng.dma_start(q_st[par][ROWS + p:ROWS + p + 1, :, :].rearrange("o h n -> o (h n)"),
                              m_parts[:, p, :]).then_inc(mrow_ok, 16)
        if has(i, 2, full):
            reached(eng, split, i + 2, 3, 3)
            q_out = a["q_scr"][bass.ds(i + 2, 1)].rearrange("o r h n -> (o r) h n")
            k_out = a["k_scr"][bass.ds(i + 2, 1)].rearrange("o r h n -> (o r) h n")
            for c, (pq, pk) in enumerate(zip(Q_PART, K_PART)):
                r = slice(c * HD, (c + 1) * HD)
                eng.dma_start(q_out[r].rearrange("d h n -> h d n"),
                              qk_parts[:, pq, 0:T]).then_inc(scr_ok, 16)
                eng.dma_start(k_out[r].rearrange("d h n -> h d n"),
                              qk_parts[0:NKV * HD, pk, T:2 * T]).then_inc(scr_ok, 16)
            reached(eng, scr_ok, i + 2, 16 * NSTK, 16 * NSTK)
            reached(eng, st_ps, i, NH, NH)
            if isinstance(i, int) and i + 2 < 2:
                eng.wait_ge(init_p, 2)
            eng.dma_start(q_st[par][0:ROWS, :, :], q_out).then_inc(stk_ok, 16)
            eng.dma_start(k_st[par][0:ROWS, :, :], k_out).then_inc(stk_ok, 16)

    def sync_start(eng):
        for c in range(4):
            n = NT // 4
            eng.dma_start(x_sb[:, c * n:(c + 1) * n, :], a["x"][:, c * n:(c + 1) * n, :]).then_inc(ld_x, 16)
        eng.dma_start(ident[:, :], a["ident"]).then_inc(ld_w, 16)
        eng.dma_start(wq[:, :], w["Wq"]).then_inc(ld_w, 16)
        for r in range(4):
            eng.dma_start(wk4[:, r, :], w["Wk"]).then_inc(ld_w, 16)
        eng.dma_start(wv[:, :], w["Wv"]).then_inc(ld_w, 16)
        eng.dma_start(w1[:, :], w["ew1"]).then_inc(ld_w, 16)
        eng.dma_start(w2[:, :, :], w["ew2"].rearrange("(k p) n -> p k n", p=P)).then_inc(ld_w, 16)
        eng.dma_start(wg[:, :], w["Wg"]).then_inc(ld_w, 16)
        eng.dma_start(wo[:, :], w["Wo"]).then_inc(ld_w, 16)
        eng.dma_start(bq_c[:, :], w["bq"].rearrange("(p o) -> p o", o=1)).then_inc(ld_w, 16)
        for dst, src in t["loads"]:
            eng.dma_start(dst, src).then_inc(done["ld1"], 16)
        steps(sync_body)(eng)

    def pe_body(eng, i, par, full=False):
        od = 1 - par
        mm = eng.matmul

        def scores(n):
            if not has(i, 1, full):
                return
            q, pair = n // (NH // 2), n % (NH // 2)
            if n == 0:
                reached(eng, stk_ok, i + 1, 32, 32)
            reached(eng, mx_ok, i + 1, NH, n - 1)
            for j in range(2):
                last = mm(s_bank[n % 2][:, j * T:(j + 1) * T],
                          q_st[od][0:ROWS, 2 * pair + j, q * P:(q + 1) * P],
                          k_st[od][0:ROWS, 2 * pair // G, :], start=True, stop=True)
            last.then_inc(s_ps, 1)

        def pv(b_par, b, grp):
            kt = grp % 2
            reached(eng, p_ok, b, NH, 4 * grp + 4)
            if grp == 0:
                reached(eng, o_ok, b, 2, 0)
                reached(eng, v_ok, b, 1, 1)
            if grp == 2:
                reached(eng, o_ok, b, 2, 1)
            for kv in range(NKV):
                last = mm(pv_bank[kv * VW:(kv + 1) * VW, :], v_sb[b_par][:, kt, kv, :],
                          pt[:, (4 * grp + kv) % 8, :], start=(kt == 0), stop=(kt == 1))
            last.then_inc(pv_ok, 1)

        def o_transposes(b, gp, dst):
            reached(eng, o_ok, b, 2, gp + 1)
            for q in range(TPB):
                for g in range(2):
                    c = q * 2 + g
                    last = eng.transpose(dst[:, c * P:(c + 1) * P],
                                         o_sb[:, gp, g * T + q * P:g * T + (q + 1) * P], ident[:, :])
            last.then_inc(ot_ps, 1)

        def ffn_in(half):
            if not has(i, 1, full):
                return
            if half == 0:
                reached(eng, xnT_ok, i + 1, 1, 1)
                reached(eng, on_ok, i - 1, 2, 1)
                reached(eng, y_ok, i, 1, 1)
            else:
                reached(eng, h_ok, i + 1, 2, 1)
            for j in range(2):
                c = 2 * half + j
                last = mm(bB[:, j * T:(j + 1) * T], w1[:, c * P:(c + 1) * P], xnT[od][:, :],
                          start=True, stop=True)
            last.then_inc(h_ps, 1)

        def ffn_out():
            if not has(i, 1, full):
                return
            reached(eng, h_ok, i + 1, 2, 2)
            for q in range(TPB):
                for c in range(KC):
                    last = mm(bB[:, q * P:(q + 1) * P], hT[:, c, q * P:(q + 1) * P], w2[:, c, :],
                              start=(c == 0), stop=(c == KC - 1))
            last.then_inc(f_ps, 1)

        def tail_heads():
            if not has(i, -1, full):
                return
            reached(eng, qk_ok, i + 2 if has(i, 2, full) else NB - 1, 1, 1)
            o_transposes(i - 1, 1, bA)

        def tail_back():
            if not has(i, -1, full):
                return
            reached(eng, on_ok, i - 1, 2, 2)
            nxt = i + 1 if has(i, 1, full) else NB - 1
            reached(eng, v_ok, nxt, 1, 1)
            reached(eng, srt_ok, nxt, 2, 2)
            if has(i, 0, full):
                reached(eng, negm_ok, i, 1, 1)
            for q in range(TPB):
                last = eng.transpose(bC[:, q * P:(q + 1) * P], on[:, q, :], ident[:, :])
            last.then_inc(oT_ps, 1)

        def tail_out():
            if not has(i, -1, full):
                return
            reached(eng, oT_ok, i - 1, 1, 1)
            for q in range(TPB):
                last = mm(bC[:, q * P:(q + 1) * P], oT[:, q * P:(q + 1) * P], wo[:, :],
                          start=True, stop=True)
            last.then_inc(w_ps, 1)

        if has(i, 0, full):
            reached(eng, mx_ok, i, NH, NH)
            reached(eng, v_ok, i, 1, 1)
            reached(eng, srt_ok, i, 2, 2)
            eng.transpose(bC[0:TPB * NH, 0:P], mx[:, :, :].rearrange("p h q -> p (h q)"),
                          ident[:, :]).then_inc(mT_ps, 1)
        if has(i, -1, full):
            pv(od, i - 1, 3)
        if has(i, 2, full):
            reached(eng, xn_ok, i + 2, 1, 1)
            reached(eng, qk_ok, i + 1, 1, 1)
            for q in range(TPB):
                last = eng.transpose(bA[:, q * P:(q + 1) * P], xn[:, q, :], ident[:, :])
            last.then_inc(xnT_ps, 1)
        ffn_in(0)
        if has(i, 2, full):
            reached(eng, xnT_ok, i + 2, 1, 1)
            mm(bA[:, 0:T], wq[:, :], xnT[par][:, :], start=True, stop=True)
            mm(bA[:, T:2 * T], wk4[:, :, :].rearrange("p r n -> p (r n)"), xnT[par][:, :],
               start=True, stop=True).then_inc(qk_ps, 1)
        scores(0)
        scores(1)
        if has(i, 1, full):
            reached(eng, negm_ok, i, 1, 1)
            for q in range(TPB):
                mm(bC[:, q * 32:(q + 1) * 32], xnT[od][:, q * P:(q + 1) * P], wv[:, :],
                   start=True, stop=True)
                last = mm(bC[:, 128 + q * NE:128 + (q + 1) * NE], xnT[od][:, q * P:(q + 1) * P],
                          wg[:, :], start=True, stop=True)
            last.then_inc(v_ps, 1)
        ffn_in(1)
        scores(2)
        scores(3)
        ffn_out()
        nxt_s = 4
        for n in range(NH):
            if has(i, 0, full):
                gp, kt, kv = n // 8, n // 4 % 2, n % 4
                if n == 0:
                    reached(eng, mrow_ok, i, 16 * NMR, 16 * NMR)
                reached(eng, p_ok, i, NH, n - 1)
                h0 = kv * G + 2 * gp
                mm(st_bank[n % 2][:, :], k_st[par][:, kv, kt * P:(kt + 1) * P],
                   q_st[par][:, h0:h0 + 2, :].rearrange("r h n -> r (h n)"),
                   start=True, stop=True).then_inc(st_ps, 1)
            if n % 4 != 3:
                scores(nxt_s)
                nxt_s += 1
            if n in (1, 4, 7):
                {1: tail_heads, 4: tail_back, 7: tail_out}[n]()
            if has(i, 0, full):
                if n == 5:
                    pv(par, i, 0)
                if n == 9:
                    pv(par, i, 1)
                if n == 13:
                    nxt = i + 1 if has(i, 1, full) else NB - 1
                    reached(eng, y_ok, nxt, 1, 1)
                    o_transposes(i, 0, bB)
                    pv(par, i, 2)

    def tensor_start(eng):
        eng.wait_ge(ld_w, 16 * NLOAD)
        steps(pe_body)(eng)

    def act_body(eng, i, par, full=False):
        od = 1 - par
        if has(i, -1, full):
            reached(eng, pv_ok, i - 1, 4, 4)
            eng.activation(o_sb[:, 1, :], pv_bank[:, :], ACT.Copy).then_inc(o_ok, 1)
        if has(i, 2, full):
            reached(eng, xnT_ps, i + 2, 1, 1)
            reached(eng, f_ps, i, 1, 1)
            reached(eng, v_ps, i, 1, 1)
            eng.activation(xnT[par][:, :], bA[:, 0:T], ACT.Copy).then_inc(xnT_ok, 1)
        if has(i, 0, full):
            reached(eng, mT_ps, i, 1, 1)
            reached(eng, msplit, i - 1, 3, 3)
            reached(eng, mrow_ok, i - 1, 16 * NMR, 16 * NMR)
            eng.activation(m_parts[:, 0, :], bC[0:TPB * NH, 0:P], ACT.Copy, scale=-1.0)
            eng.activation(negm[:, :], bC[0:TPB * NH, 0:P], ACT.Copy, scale=-1.0).then_inc(negm_ok, 1)

        def relu(half):
            if has(i, 1, full):
                reached(eng, h_ps, i + 1, 2, half + 1)
                reached(eng, f_ps, i, 1, 1)
                eng.activation(hT[:, 2 * half:2 * half + 2, :],
                               bB[:, :].rearrange("p (c n) -> p c n", c=2), ACT.Relu).then_inc(h_ok, 1)

        relu(0)
        if has(i, 2, full):
            reached(eng, qk_ps, i + 2, 1, 1)
            reached(eng, split, i + 1, 3, 3)
            reached(eng, scr_ok, i + 1, 16 * NSTK, 16 * NSTK)
            for half, bias in ((0, bq_c), (1, bk_c)):
                c = slice(half * T, (half + 1) * T)
                eng.activation(qk[:, c], bA[:, c], ACT.Identity, bias=bias[:, 0:1])
                last = eng.activation(qk_parts[:, 0, c], bA[:, c], ACT.Identity, bias=bias[:, 0:1])
            last.then_inc(qk_ok, 1)
        relu(1)
        if has(i, 1, full):
            reached(eng, gch, i + 1, NGC, 1)
            reached(eng, gch, i, NGC, NGC)
            eng.activation(gex[:, :, :], gd[:, :, :], ACT.Exp).then_inc(gex_ok, 1)
        for n in range(NH):
            if has(i, 0, full):
                reached(eng, st_ps, i, NH, n + 1)
                if n % 4 == 0:
                    reached(eng, pv_ok, i, 4, n // 4 - 1)
                eng.activation(pt[:, n % 8, :], st_bank[n % 2][:, :], ACT.Exp,
                               scale=HD ** -0.5).then_inc(p_ok, 1)
                if n == 10:
                    reached(eng, pv_ok, i, 4, 2)
                    reached(eng, ot_ps, i - 1, 2, 1)
                    eng.activation(o_sb[:, 0, :], pv_bank[:, :], ACT.Copy).then_inc(o_ok, 1)

    def scalar_start(eng):
        eng.dma_start(bo_bc[:, :], a["bo_bc"]).then_inc(ld_row, 16)
        eng.dma_start(bv_bc[:, :], a["bv_bc"]).then_inc(ld_row, 16)
        for r in range(4):
            n = NKV * HD
            eng.dma_start(bk_c[r * n:(r + 1) * n, :], w["bk"].rearrange("(p o) -> p o", o=1)).then_inc(ld_row, 16)
        eng.wait_ge(st_mv, 2)
        eng.activation(std[:, :], t["veps"][:, :], ACT.Sqrt).then_inc(st_sd, 1)
        eng.wait_ge(ld_w, 16 * NLOAD)
        eng.wait_ge(ld_row, 16 * 6)
        steps(act_body)(eng)

    def dve_body(eng, i, par, full=False):
        od = 1 - par

        def maxima(n):
            if not has(i, 1, full):
                return
            q, pair = n // (NH // 2), n % (NH // 2)
            reached(eng, s_ps, i + 1, NH, n + 1)
            if n == 0:
                reached(eng, mT_ps, i, 1, 1)
            eng.tensor_reduce(mx[:, 2 * pair:2 * pair + 2, q], s_bank[n % 2][:, :].rearrange("p (h k) -> p h k", h=2),
                              AX.X, ALU.max).then_inc(mx_ok, 1)

        def heads(b, gp, src):
            reached(eng, ot_ps, b, 2, gp + 1)
            v = src[:, :].rearrange("p (q c w) -> p q c w", q=TPB, w=VW)
            r = rden[:, gp, :].rearrange("p (q c o) -> p q c o", q=TPB, o=1)
            eng.reciprocal(r, v[:, :, :, HD:HD + 1]).then_inc(rd_ok, 1)
            reached(eng, rd_ok, b, 2, gp + 1)
            half = on[:, :, gp * P // 2:(gp + 1) * P // 2]
            eng.tensor_tensor(half.rearrange("p q (c d) -> p q c d", d=HD), v[:, :, :, 0:HD],
                              r.broadcast_to([P, TPB, NH // 2, HD]), ALU.mult).then_inc(on_ok, 1)

        maxima(0)
        maxima(1)
        if has(i, 1, full):
            reached(eng, v_ps, i + 1, 1, 1)
            reached(eng, pv_ok, i - 1, 4, 4)
            reached(eng, gch, i, NGC, 1)
            eng.tensor_tensor(v_sb[od][:, :, :, 0:HD],
                              bC[:, 0:64].rearrange("p (q k d) -> p q k d", q=TPB, k=NKV),
                              bv_bc[:, :].rearrange("p (o k d) -> p o k d", o=1, k=NKV)
                              .broadcast_to([P, TPB, NKV, HD]), ALU.add).then_inc(v_ok, 1)
            for q in range(TPB):
                eng.max(srt[:, q, :], bC[:, 128 + q * NE:128 + (q + 1) * NE]).then_inc(srt_ok, 1)
        for n in range(2, 5):
            maxima(n)
        if has(i, -1, full):
            heads(i - 1, 1, bA)
        maxima(5)
        maxima(6)
        if has(i, -1, full):
            reached(eng, oT_ps, i - 1, 1, 1)
            eng.tensor_copy(oT[:, :], bC[:, 0:T]).then_inc(oT_ok, 1)
        maxima(7)
        maxima(8)
        maxima(9)
        if has(i, -1, full):
            reached(eng, w_ps, i - 1, 1, 1)
            reached(eng, y_ok, i - 1, 1, 1)
            tile0 = (i - 1) * TPB
            eng.tensor_tensor(x1[:, bass.ds(tile0, TPB), :], xb_sb[:, bass.ds(tile0, TPB), :],
                              bC[:, 0:T].rearrange("p (q n) -> p q n", q=TPB), ALU.add).then_inc(x1_ok, 1)
            reached(eng, x1_ok, i - 1, 1, 1)
            for q in range(TPB):
                eng.bn_stats(t["bst1"][:, bass.ds(tile0 + q, 1), :].rearrange("p o s -> p (o s)"),
                             x1[:, bass.ds(tile0 + q, 1), :].rearrange("p o n -> p (o n)")).then_inc(done["bn1"], 1)
        for n in range(10, 14):
            maxima(n)
            if n in (11, 13) and has(i, 1, full):
                src, dst, step = (gz, grz, 4) if n == 11 else (gm, grm, 6)
                reached(eng, gch, i + 1, NGC, step)
                if n == 13:
                    eng.tensor_scalar(gm[:, :, :], gs[:, :, :], F32_EPS, None, ALU.max).then_inc(gr_ok, 1)
                    reached(eng, gr_ok, i + 1, 3, 2)
                eng.reciprocal(dst[:, :, :], src[:, :, :]).then_inc(gr_ok, 1)
        if has(i, 1, full):
            reached(eng, f_ps, i + 1, 1, 1)
            reached(eng, gch, i + 1, NGC, NGC)
            for q in range(TPB):
                row = xb_sb[:, bass.ds((i + 1) * TPB + q, 1), :].rearrange("p o n -> p (o n)")
                last = eng.scalar_tensor_tensor(row, bB[:, q * P:(q + 1) * P], gate[:, q, 0:1], row,
                                                ALU.mult, ALU.add)
            last.then_inc(y_ok, 1)
        for n in range(14, 16):
            maxima(n)
        if has(i, 0, full):
            heads(i, 0, bB)
        if has(i, 3, full):
            reached(eng, xnT_ps, i + 2, 1, 1)
            for q in range(TPB):
                c = (i + 3) * TPB + q
                last = eng.tensor_scalar(xn[:, q, :], x_sb[:, bass.ds(c, 1), :].rearrange("p o n -> p (o n)"),
                                         mv[:, bass.ds(c, 1), 0:1].rearrange("p o s -> p (o s)"),
                                         rstd[:, bass.ds(c, 1)], ALU.subtract, ALU.mult)
            last.then_inc(xn_ok, 1)

    def vector_start(eng):
        for p in range(2):
            eng.memset(v_sb[p][:, :, :, :], 0.0).then_inc(done["dv"], 1)
        eng.wait_ge(done["dv"], 2)
        for p in range(2):
            eng.memset(v_sb[p][:, :, :, HD:HD + 1], 1.0).then_inc(v_init := done["dv"], 1)
        for c in range(NT):
            if c % (NT // 4) == 0:
                eng.wait_ge(ld_x, 16 * 4)
            eng.bn_stats(bst[:, c, :], x_sb[:, c, :]).then_inc(st_bn, 1)
        eng.wait_ge(st_bn, NT)
        for c in range(NT):
            last = eng.bn_aggr(mv[:, c, :], bst[:, c, :])
        last.then_inc(st_mv, 1)
        eng.wait_ge(st_mv, 1)
        eng.tensor_scalar(t["veps"][:, :], mv[:, :, 1], LN_EPS, None, ALU.add).then_inc(st_mv, 1)
        eng.wait_ge(st_sd, 1)
        eng.reciprocal(rstd[:, :], std[:, :]).then_inc(st_rs, 1)
        eng.wait_ge(st_rs, 1)
        eng.wait_ge(done["dv"], 4)
        eng.wait_ge(ld_row, 16 * 6)
        eng.wait_ge(xb_ok, 1)
        steps(dve_body)(eng)

    def pool_body(eng, i, par, full=False):
        TT = eng.tensor_tensor
        if has(i, 0, full):
            reached(eng, negm_ok, i, 1, 1)
            TT(negm_rest[:, :], negm[:, :], m_parts[:, 0, :], ALU.subtract).then_inc(msplit, 1)
            TT(m_parts[:, 1, :], negm[:, :], m_parts[:, 0, :], ALU.subtract).then_inc(msplit, 1)
            reached(eng, msplit, i, 3, 2)
            TT(m_parts[:, 2, :], negm_rest[:, :], m_parts[:, 1, :], ALU.subtract).then_inc(msplit, 1)
        if has(i, 1, full):
            reached(eng, srt_ok, i + 1, 2, 2)
            reached(eng, gex_ok, i, 1, 1)
            TT(gd[:, :, :], srt[:, :, :], srt[:, :, 0:1].broadcast_to([P, TPB, NE]),
               ALU.subtract).then_inc(gch, 1)
        if has(i, 2, full):
            reached(eng, qk_ok, i + 2, 1, 1)
            TT(qk_rest[:, :], qk[:, :], qk_parts[:, 0, :], ALU.subtract).then_inc(split, 1)
            TT(qk_parts[:, 1, :], qk[:, :], qk_parts[:, 0, :], ALU.subtract).then_inc(split, 1)
            reached(eng, split, i + 2, 3, 2)
            TT(qk_parts[:, 2, :], qk_rest[:, :], qk_parts[:, 1, :], ALU.subtract).then_inc(split, 1)
        if has(i, 1, full):
            b = i + 1
            reached(eng, gex_ok, b, 1, 1)
            chain = [
                lambda: TT(g4[:, :, :], gex[:, :, 0:4], gex[:, :, 4:8], ALU.add),
                lambda: TT(g2[:, :, :], g4[:, :, 0:2], g4[:, :, 2:4], ALU.add),
                lambda: TT(gz[:, :, :], g2[:, :, 0:1], g2[:, :, 1:2], ALU.add),
                lambda: TT(gp2[:, :, :], gex[:, :, 0:2], grz[:, :, :].broadcast_to([P, TPB, 2]), ALU.mult),
                lambda: TT(gs[:, :, :], gp2[:, :, 0:1], gp2[:, :, 1:2], ALU.add),
                lambda: TT(gq[:, :, :], gp2[:, :, :], grm[:, :, :].broadcast_to([P, TPB, 2]), ALU.mult),
                lambda: TT(gate[:, :, :], gq[:, :, 0:1], gq[:, :, 1:2], ALU.add),
            ]
            for k, op in enumerate(chain):
                if k in (3, 5):
                    reached(eng, gr_ok, b, 3, 1 if k == 3 else 3)
                if k == len(chain) - 1:
                    reached(eng, y_ok, b - 1, 1, 1)
                op().then_inc(gch, 1)
                reached(eng, gch, b, NGC, k + 2)

    def gpsimd_start(eng):
        for p in range(2):
            eng.memset(k_st[p][:, :, :], 1.0).then_inc(init_p, 1)
        eng.wait_ge(ld_x, 16 * 4)
        eng.wait_ge(ld_row, 16 * 6)
        eng.tensor_tensor(xb_sb[:, :, :], x_sb[:, :, :],
                          bo_bc[:, :].rearrange("p (o n) -> p o n", o=1).broadcast_to([P, NT, P]),
                          ALU.add).then_inc(xb_ok, 1)
        steps(pool_body)(eng)

    bodies = dict(sync=sync_body, tensor=pe_body, scalar=act_body, vector=dve_body, gpsimd=pool_body)
    starts = dict(sync=sync_start, tensor=tensor_start, scalar=scalar_start, vector=vector_start,
                  gpsimd=gpsimd_start)
    return starts, {n: (lambda eng, body=body: body(eng, NB, NB % 2)) for n, body in bodies.items()}


def early_buffers(sb):
    n_tok = NB * T
    return dict(
        mv1=sb("mv1", [P, NT, 2]), std1=sb("std1", [P, NT]), rstd1=sb("rstd1", [P, NT]),
        w3s=sb("w3s", [P, KC, P]),
        nega=sb("nega", [P, CI, NS]),
        wx_p=sb("wx_p", [P, CI, NPART * 32]),
        sel=sb("sel", [NPART * 32, NS, P], BF16),
        xn1=sb("xn1", [P, NT, P]), xnT1=sb("xnT1", [P, n_tok]),
        xc=sb("xc", [P, CI, GT]),
        xs=sb("xs", [P, CI, n_tok]), zs=sb("zs", [P, CI, n_tok]))


def layer1(nc, sb, sem, banks, w, t, early, done, out):
    NTOK = NB * T
    x1, ident, bst1 = t["x1"], t["ident"], t["bst1"]
    (win, wdt, wx, wout, w1, w2, h1, h2, w3) = (t[n] for n in
        ("win", "wdt", "wx", "wout", "f1", "f2", "fh1", "fh2", "f3"))
    mv, std, rstd, w3s, nega, wx_p, sel, xn, xnT, xc, xs, zs = (early[n] for n in
        ("mv1", "std1", "rstd1", "w3s", "nega", "wx_p", "sel", "xn1", "xnT1", "xc", "xs", "zs"))
    sil = sb("sil", [P, KC, GT])
    g2 = sb("gelu2", [P, KC, GT])
    g3 = sb("gelu3", [P, KC, GT])
    dt = sb("dt", [P, CI, GT])
    u_abs, u_pos = sb("u_abs", [P, CI, GT]), sb("u_pos", [P, CI, GT])
    e_sb, l_sb = sb("e_sb", [P, CI, GT]), sb("l_sb", [P, CI, GT])
    b_full, b_rest = sb("b_full", [NPART * 32, GT]), sb("b_rest", [NPART * 32, GT])
    b_mid = sb("b_mid", [NPART * 32, GT], BF16)
    b_parts = sb("b_parts", [NPART * 32, NTOK], BF16)
    NR, NRD = 8, 16
    da = sb("da", [P, NRD, GB, T])
    hb = sb("hb", [P, NR, GT])
    acc = sb("acc", [P, CI, GT])
    y = sb("y", [P, CI, GT])
    o = sb("o", [P, GTT, P])

    pA, pB = banks[0:2]
    f_bank = [banks[6], banks[2], banks[3], banks[5]]
    b_bank = [banks[4], banks[7]]

    (i_act, da_zero, st_ok, sd_ok, i_pool, xn_ok, xT_ps, xT_ok, l1_ps, sil_ok, h0_ok, win_ps, z_ok, cv_ok, conv, xs_ok,
     dt_ps, u_ok, sp_ok, spd, bx_ps, bx_ok, bsp, b_ps, da_ok, scan, acc0, acc1, y_ok, l2_ps, g2_ok,
     l3_ps, g3_ok, o_ps, o_ok, out_ok, acc1_0) = [sem("b_" + n) for n in (
         "i_act", "da_zero", "st_ok", "sd_ok", "i_pool", "xn_ok", "xT_ps", "xT_ok", "l1_ps", "sil_ok", "h0_ok", "win_ps",
         "z_ok", "cv_ok", "conv", "xs_ok", "dt_ps", "u_ok", "sp_ok", "spd", "bx_ps", "bx_ok", "bsp",
         "b_ps", "da_ok", "scan", "acc0", "acc1", "y_ok", "l2_ps", "g2_ok", "l3_ps", "g3_ok", "o_ps",
         "o_ok", "out_ok", "acc1_0")]
    NSP = 4
    NPI = 6
    PARTS = ((0, NT - GTT), (NT - GTT, NT))

    def steps(body):
        def run(eng, last_of_layer0):
            body(eng, -1, between=last_of_layer0)
            body(eng, 0)
            with eng.Fori(1, NG - 1) as g:
                body(eng, g, full=True)
            body(eng, NG - 1)
            body(eng, NG)
        return run

    def has(g, off, full):
        return full or 0 <= g + off < NG

    def cols(g):
        return bass.ds(g * GT, GT)

    def sync_body(eng, g, full=False, between=None):
        if between:
            between(eng)
        if has(g, -1, full):
            reached(eng, o_ok, g - 1, 1, 1)
            eng.dma_start(out[:, bass.ds((g - 1) * GTT, GTT), :], o[:, :, :]).then_inc(out_ok, 16)

    def sync_all(eng, last_of_layer0):
        steps(sync_body)(eng, last_of_layer0)
        eng.wait_ge(out_ok, 16 * NG)

    def pe_body(eng, g, full=False, between=None):
        mm = eng.matmul
        nx, cur, prv = has(g, 1, full), has(g, 0, full), has(g, -1, full)
        state = [0]

        def b_row(keep=False):
            s = state[0]
            if not cur or s >= NS:
                return
            state[0] += 1
            if s == 0:
                reached(eng, bsp, g, 4, 4)
            reached(eng, scan, g, 2 * NS, 2 * (s - 1))
            mm(b_bank[s % 2][:, :], sel[:, s, :], b_parts[:, cols(g)], start=True,
               stop=True).then_inc(b_ps, 1)

        def ffn1(c):
            if not cur:
                return
            fa, fb = f_bank[2 * (c % 2)], f_bank[2 * (c % 2) + 1]
            if c < 2:
                reached(eng, g3_ok, g - 1, KC, 2 * c + 2)
                reached(eng, xT_ok, g, 1, 1)
            else:
                reached(eng, h0_ok, g, KC, c - 1)
            mm(fa[:, :], w1[:, c * P:(c + 1) * P], xnT[:, cols(g)], start=True, stop=True)
            mm(fb[:, :], w2[:, c * P:(c + 1) * P], xnT[:, cols(g)], start=True, stop=True).then_inc(l1_ps, 1)

        def w_in(c, dst):
            if nx:
                mm(dst[:, :], win[:, c * P:(c + 1) * P], xnT[:, cols(g + 1)], start=True,
                   stop=True).then_inc(win_ps, 1)

        def hidden(c, wt, src, ready, free, done_sem):
            if not cur:
                return
            for k in range(KC):
                reached(eng, ready, g, KC, k + 1)
                if k == 0:
                    reached(eng, *free)
                last = mm(f_bank[c][:, :], wt[:, k, c * P:(c + 1) * P], src[:, k, :],
                          start=(k == 0), stop=(k == KC - 1))
                if k % 2:
                    b_row() if k < KC - 1 else None
            last.then_inc(done_sem, 1)
            b_row()

        def transposes(b):
            eng.wait_ge(xn_ok, b + 1)
            for q in range(GTT):
                last = eng.transpose(f_bank[b][:, q * P:(q + 1) * P], xn[:, b * GTT + q, :], ident[:, :])
            last.then_inc(xT_ps, 1)

        prologue = isinstance(g, int) and g < 0
        if prologue:
            between(eng)
            transposes(0)
        b_row()
        b_row()
        ffn1(0)
        ffn1(1)
        if nx:
            reached(eng, u_ok, g, 4, 4)
            reached(eng, xT_ok, g + 1, 1, 1)
            w_in(0, pB)
            w_in(1, pA)
        if prologue:
            for b in range(1, NG):
                transposes(b)
        ffn1(2)
        ffn1(3)
        if nx:
            reached(eng, conv, g + 1, 6, 3)
            w_in(2, pB)
            reached(eng, conv, g + 1, 6, 6)
            w_in(3, pA)
        if prv:
            if nx:
                reached(eng, z_ok, g + 1, 2, 1)
            else:
                reached(eng, u_ok, NG - 1, 4, 4)
            reached(eng, y_ok, g - 1, 2, 2)
            reached(eng, g3_ok, g - 1, KC, KC)
            for q in range(GTT):
                r = slice(q * P, (q + 1) * P)
                for k in range(KC):
                    mm(pB[:, r], g3[:, k, r], w3s[:, k, :], start=(k == 0), stop=False)
                for c in range(CI):
                    last = mm(pB[:, r], y[:, c, r], wout[:, c, :], start=False, stop=(c == CI - 1))
            last.then_inc(o_ps, 1)

        def second(c):
            hidden(c, h1, sil, h0_ok, (h0_ok, g, KC, 3 if c < 2 else 4), l2_ps)

        if nx:
            reached(eng, xs_ok, g + 1, 2, 2)
            reached(eng, z_ok, g + 1, 2, 2)
            for c in range(CI):
                last = mm(pA[0:NPART * 32, :], wx_p[:, c, :], xs[:, c, cols(g + 1)],
                          start=(c == 0), stop=(c == CI - 1))
            last.then_inc(bx_ps, 1)
        b_row()
        second(0)
        second(1)

        def step_in(c, dst, *free):
            if nx:
                reached(eng, *free)
                for k in range(CI):
                    last = mm(dst[:, :], wdt[:, k, c * P:(c + 1) * P], xs[:, k, cols(g + 1)],
                              start=(k == 0), stop=(k == CI - 1))
                last.then_inc(dt_ps, 1)
            b_row()

        step_in(0, pA, bx_ok, g + 1, 1, 1)
        second(2)
        step_in(1, pB, o_ok, g - 1, 1, 1)
        second(3)
        for c in range(KC):
            hidden(c, h2, g2, g2_ok, (g2_ok, g, KC, c + 1), l3_ps)
        while cur and state[0] < NS:
            b_row()

    def tensor_all(eng, last_of_layer0):
        eng.wait_ge(done["ld1"], 16 * len(t["loads"]))
        eng.wait_ge(i_pool, NPI)
        steps(pe_body)(eng, last_of_layer0)

    def deviation(eng, part):
        lo, hi = PARTS[part]
        eng.wait_ge(st_ok, 2 * part + 2)
        eng.activation(std[:, lo:hi], t["veps"][:, lo:hi], ACT.Sqrt).then_inc(sd_ok, 1)

    def act_body(eng, g, full=False, between=None):
        nx, cur, prv = has(g, 1, full), has(g, 0, full), has(g, -1, full)
        act = eng.activation
        def xnt_out(b):
            eng.wait_ge(xT_ps, b + 1)
            act(xnT[:, b * GT:(b + 1) * GT], f_bank[b][:, :], ACT.Copy).then_inc(xT_ok, 1)

        prologue = isinstance(g, int) and g < 0
        if prologue:
            between(eng)
            deviation(eng, 1)
            xnt_out(0)

        def ffn_silu(c):
            if cur:
                reached(eng, l1_ps, g, KC, c + 1)
                reached(eng, l2_ps, g - 1, KC, KC)
                act(sil[:, c, :], f_bank[2 * (c % 2)][:, :], ACT.Silu,
                    scale=t["f1s"][:, c:c + 1]).then_inc(sil_ok, 1)

        def taps(c, src):
            reached(eng, win_ps, g + 1, 4, c + 1)
            reached(eng, xs_ok, g, 2, 2)
            act(xc[:, c, :], src[:, :], ACT.Identity, bias=t["cb"][:, c:c + 1],
                scale=t["cw"][:, c, TAPS - 1:TAPS]).then_inc(cv_ok, 1)

        def gate_z(c, src):
            reached(eng, win_ps, g + 1, 4, c + 3)
            settled(eng, i_pool, NPI)
            act(zs[:, c, cols(g + 1)], src[:, :], ACT.Silu).then_inc(z_ok, 1)

        def gate_x(c):
            reached(eng, conv, g + 1, 6, 3 * c + 3)
            settled(eng, i_pool, NPI)
            act(xs[:, c, cols(g + 1)], xc[:, c, :], ACT.Silu).then_inc(xs_ok, 1)

        ffn_silu(0)
        ffn_silu(1)
        if nx:
            taps(0, pB)
            taps(1, pA)
        ffn_silu(2)
        ffn_silu(3)
        if nx:
            gate_x(0)
            gate_z(0, pB)
            gate_x(1)
            gate_z(1, pA)
        if prologue:
            for b in range(1, NG):
                xnt_out(b)

        def decay(s):
            if not cur:
                return
            if s == 0:
                reached(eng, spd, g, NSP, NSP)
            for c in range(CI):
                n = CI * s + c
                reached(eng, scan, g, 2 * NS, n + 1 - NRD)
                act(da[:, n % NRD, :, 1:T],
                    dt[:, c, :].rearrange("p (b n) -> p b n", b=GB)[:, :, 1:T],
                    ACT.Exp, scale=nega[:, c, s:s + 1]).then_inc(da_ok, 1)

        def dt_in(c, src):
            if nx:
                reached(eng, dt_ps, g + 1, 2, c + 1)
                reached(eng, spd, g, NSP, NSP)
                act(u_abs[:, c, :], src[:, :], ACT.Abs, bias=t["bdt"][:, c:c + 1]).then_inc(u_ok, 1)
                act(u_pos[:, c, :], src[:, :], ACT.Relu, bias=t["bdt"][:, c:c + 1]).then_inc(u_ok, 1)

        def b_in():
            if nx:
                reached(eng, bx_ps, g + 1, 1, 1)
                reached(eng, bsp, g, 4, 4)
                settled(eng, i_pool, NPI)
                act(b_parts[:, cols(g + 1)], pA[0:NPART * 32, :], ACT.Copy)
                act(b_full[:, :], pA[0:NPART * 32, :], ACT.Copy).then_inc(bx_ok, 1)

        for s in range(NS):
            decay(s)
            if s == 8:
                b_in()
        dt_in(0, pA)
        dt_in(1, pB)
        if cur:
            for c in range(KC):
                reached(eng, l2_ps, g, KC, c + 1)
                reached(eng, l3_ps, g - 1, KC, KC)
                act(g2[:, c, :], f_bank[c][:, :], ACT.Gelu, scale=t["h1s"][:, c:c + 1]).then_inc(g2_ok, 1)
        if nx:
            reached(eng, u_ok, g + 1, 4, 4)
            act(e_sb[:, :, :], u_abs[:, :, :], ACT.Exp, scale=-1.0).then_inc(sp_ok, 1)
            reached(eng, spd, g + 1, NSP, 1)
            act(l_sb[:, :, :], u_abs[:, :, :], ACT.Ln).then_inc(sp_ok, 1)
        if cur:
            for c in range(KC):
                reached(eng, l3_ps, g, KC, c + 1)
                reached(eng, o_ps, g - 1, 1, 1)
                act(g3[:, c, :], f_bank[c][:, :], ACT.Gelu, scale=t["h2s"][:, c:c + 1]).then_inc(g3_ok, 1)

    def scalar_all(eng, last_of_layer0):
        eng.wait_ge(done["ld1"], 16 * len(t["loads"]))
        eng.activation(nega[:, :, :], t["alog"][:, :, :], ACT.Exp).then_inc(i_act, 1)
        eng.wait_ge(i_act, 1)
        eng.activation(nega[:, :, :], nega[:, :, :], ACT.Copy, scale=-1.0).then_inc(i_act, 1)
        eng.wait_ge(i_act, 2)
        eng.wait_ge(i_pool, NPI)
        deviation(eng, 0)
        steps(act_body)(eng, last_of_layer0)

    def dve_body(eng, g, full=False, between=None):
        nx, cur, prv = has(g, 1, full), has(g, 0, full), has(g, -1, full)
        STT = eng.scalar_tensor_tensor

        def ffn_mul(c):
            if cur:
                reached(eng, sil_ok, g, KC, c + 1)
                STT(sil[:, c, :], f_bank[2 * (c % 2) + 1][:, :], t["f2s"][:, c:c + 1], sil[:, c, :],
                    ALU.mult, ALU.mult).then_inc(h0_ok, 1)

        if between:
            between(eng)
            eng.memset(da[:, :, :, 0:1], 0.0).then_inc(da_zero, 1)
            eng.wait_ge(da_zero, 1)
            statistics(eng, 1)
            eng.wait_ge(sd_ok, 2)
            eng.reciprocal(rstd[:, :], std[:, :]).then_inc(st_ok, 1)
            eng.wait_ge(st_ok, 5)
            eng.wait_ge(i_pool, NPI)
            for b in range(NG):
                normalise(eng, b)
        ffn_mul(0)
        ffn_mul(1)
        for c, src in ((0, pB), (1, pA)):
            if nx:
                acc_v = xc[:, c, :].rearrange("p (b n) -> p b n", b=GB)
                src_v = src[:, :].rearrange("p (b n) -> p b n", b=GB)
                reached(eng, cv_ok, g + 1, 2, c + 1)
                for k in range(1, TAPS):
                    if k > 1:
                        reached(eng, conv, g + 1, 6, 3 * c + k - 1)
                    STT(acc_v[:, :, k:T], src_v[:, :, 0:T - k], t["cw"][:, c, TAPS - 1 - k:TAPS - k],
                        acc_v[:, :, k:T], ALU.mult, ALU.add).then_inc(conv, 1)
            ffn_mul(2 + c)
        for s in range(NS):
            if cur:
                reached(eng, b_ps, g, NS, s + 1)
                for c in range(CI):
                    n = CI * s + c
                    reached(eng, da_ok, g, 2 * NS, n + 1)
                    if c == 1:
                        reached(eng, acc1, g, NS - 1, s - NR // CI)
                    eng.tensor_tensor_scan(hb[:, n % NR, :],
                                           da[:, n % NRD, :, :].rearrange("p b n -> p (b n)"),
                                           b_bank[s % 2][:, :], 0.0, ALU.mult, ALU.add).then_inc(scan, 1)
                if s == 0:
                    reached(eng, scan, g, 2 * NS, 2)
                    for c in range(CI):
                        reached(eng, y_ok, g - 1, 2, c + 1)
                        STT(acc[:, c, :], xs[:, c, cols(g)], t["D"][:, c:c + 1], hb[:, c, :],
                            ALU.mult, ALU.add).then_inc((acc0, acc1_0)[c], 1)
                else:
                    reached(eng, scan, g, 2 * NS, 2 * s + 1)
                    reached(eng, acc0, g, NS, s)
                    eng.tensor_tensor(acc[:, 0, :], acc[:, 0, :], hb[:, CI * s % NR, :],
                                      ALU.add).then_inc(acc0, 1)
            if s == 3 and prv:
                reached(eng, o_ps, g - 1, 1, 1)
                reached(eng, out_ok, g - 2, 16, 16)
                eng.tensor_tensor(o[:, :, :], x1[:, bass.ds((g - 1) * GTT, GTT), :],
                                  pB[:, :].rearrange("p (q n) -> p q n", q=GTT), ALU.add).then_inc(o_ok, 1)
        if nx:
            mid, top = slice(32, 64), slice(64, 96)
            reached(eng, bsp, g + 1, 4, 2)
            eng.tensor_copy(b_parts[mid, cols(g + 1)], b_mid[mid, :]).then_inc(bsp, 1)
            eng.tensor_tensor(b_parts[top, cols(g + 1)], b_rest[top, :], b_mid[top, :],
                              ALU.subtract).then_inc(bsp, 1)
        if nx:
            reached(eng, sp_ok, g + 1, 2, 1)
            eng.tensor_scalar(u_abs[:, :, :], e_sb[:, :, :], 1.0, None, ALU.add).then_inc(spd, 1)
            reached(eng, spd, g + 1, NSP, 1)
            STT(e_sb[:, :, :], u_abs[:, :, :], -1.0, e_sb[:, :, :], ALU.add, ALU.subtract).then_inc(spd, 1)
            reached(eng, spd, g + 1, NSP, 2)
            eng.tensor_tensor(e_sb[:, :, :], u_pos[:, :, :], e_sb[:, :, :], ALU.subtract).then_inc(spd, 1)
            reached(eng, spd, g + 1, NSP, 3)
            reached(eng, sp_ok, g + 1, 2, 2)
            eng.tensor_tensor(dt[:, :, :], e_sb[:, :, :], l_sb[:, :, :], ALU.add).then_inc(spd, 1)
        if cur:
            for c in range(CI):
                reached(eng, acc0 if c == 0 else acc1, g, NS - c, NS - c)
                reached(eng, o_ps, g - 1, 1, 1)
                eng.tensor_tensor(y[:, c, :], acc[:, c, :], zs[:, c, cols(g)], ALU.mult).then_inc(y_ok, 1)

    def normalise(eng, g):
        for c in range(g * GTT, (g + 1) * GTT):
            last = eng.tensor_scalar(xn[:, c, :], x1[:, c, :], mv[:, c, 0:1], rstd[:, c:c + 1],
                                     ALU.subtract, ALU.mult)
        last.then_inc(xn_ok, 1)

    def statistics(eng, part):
        lo, hi = PARTS[part]
        eng.wait_ge(done["bn1"], hi)
        for c in range(lo, hi):
            last = eng.bn_aggr(mv[:, c, :], bst1[:, c, :])
        last.then_inc(st_ok, 1)
        eng.wait_ge(st_ok, 2 * part + 1)
        eng.tensor_scalar(t["veps"][:, lo:hi], mv[:, lo:hi, 1], LN_EPS, None, ALU.add).then_inc(st_ok, 1)

    def vector_all(eng, last_of_layer0):
        statistics(eng, 0)
        steps(dve_body)(eng, last_of_layer0)

    def pool_body(eng, g, full=False, between=None):
        TT = eng.tensor_tensor
        if between:
            between(eng)
        if has(g, 0, full):
            for s in range(1, NS):
                reached(eng, scan, g, 2 * NS, 2 * s + 2)
                if s == 1:
                    reached(eng, acc1_0, g, 1, 1)
                else:
                    reached(eng, acc1, g, NS - 1, s - 1)
                TT(acc[:, 1, :], acc[:, 1, :], hb[:, (CI * s + 1) % NR, :], ALU.add).then_inc(acc1, 1)
                if s == 10:
                    parts(eng, g + 1, has(g, 1, full))
        else:
            parts(eng, g + 1, has(g, 1, full))

    def parts(eng, g, on):
        if not on:
            return
        TT = eng.tensor_tensor
        reached(eng, bx_ok, g, 1, 1)
        settled(eng, i_pool, NPI)
        TT(b_rest[:, :], b_full[:, :], b_parts[:, cols(g)], ALU.subtract).then_inc(bsp, 1)
        TT(b_mid[:, :], b_full[:, :], b_parts[:, cols(g)], ALU.subtract).then_inc(bsp, 1)

    def gpsimd_all(eng, last_of_layer0):
        eng.wait_ge(done["ld1"], 16 * len(t["loads"]))
        eng.memset(wx_p[:, :, :], 0.0).then_inc(i_pool, 1)
        eng.wait_ge(i_pool, 1)
        for p in range(NPART):
            eng.tensor_copy(wx_p[:, :, 32 * p:32 * p + NS], wx[:, :, :]).then_inc(i_pool, 1)
        eng.tensor_copy(sel[:, :, :], t["pick"][:, :].rearrange("p (s o) -> p s o", o=1)
                        .broadcast_to([NPART * 32, NS, P])).then_inc(i_pool, 1)
        eng.tensor_tensor(w3s[:, :, :], w3[:, :, :],
                          t["w3s_bc"][:, :].rearrange("p (o n) -> p o n", o=1).broadcast_to([P, KC, P]),
                          ALU.mult).then_inc(i_pool, 1)
        steps(pool_body)(eng, last_of_layer0)

    return dict(sync=sync_all, tensor=tensor_all, scalar=scalar_all, vector=vector_all, gpsimd=gpsimd_all)


def program(nc, w, scr, out):
    x = w["x"].rearrange("b (q p) d -> p (b q) d", p=P)
    out = out.rearrange("b (q p) d -> p (b q) d", p=P)
    ctx = ExitStack()
    with ctx:
        def sb(name, shape, dt=F32):
            return ctx.enter_context(nc.sbuf_tensor(name, shape, dt))

        def sem(name):
            return ctx.enter_context(nc.semaphore(name))

        t = dict(ident=sb("ident", [P, P]), x1=sb("x1", [P, NT, P]), veps=sb("veps", [P, NT]),
                 bst1=sb("bst1", [P, NT, 6]))
        loads = []

        def load(name, shape, src):
            t[name] = sb("ld_" + name, shape)
            loads.append((t[name][tuple(slice(None) for _ in shape)], src))

        chunks = "(k p) n -> p k n"
        load("win", [P, 2 * DI], w["W_in"])
        load("wdt", [P, CI, DI], w["W_dt"].rearrange(chunks, p=P))
        load("wx", [P, CI, NS], w["W_x"].rearrange(chunks, p=P))
        load("wout", [P, CI, P], w["W_out"].rearrange(chunks, p=P))
        load("cw", [P, CI, TAPS], w["conv_w"].rearrange("(k p) o n -> p k (o n)", p=P))
        load("cb", [P, CI], w["conv_b"])
        load("alog", [P, CI, NS], w["A_log"].rearrange(chunks, p=P))
        load("D", [P, CI], w["D"])
        load("bdt", [P, CI], w["b_dt"])
        load("f1", [P, DFF], w["w1_t"])
        load("f2", [P, DFF], w["w2_t"])
        load("fh1", [P, KC, DFF], w["h1_t"].rearrange(chunks, p=P))
        load("fh2", [P, KC, DFF], w["h2_t"].rearrange(chunks, p=P))
        load("f3", [P, KC, P], w["w3_t"].rearrange(chunks, p=P))
        for n in ("w1", "w2", "h1", "h2"):
            load({"w1": "f1s", "w2": "f2s", "h1": "h1s", "h2": "h2s"}[n], [P, KC], w[n + "_s"])
        load("w3s_bc", [P, P], w["w3_s"].partition_broadcast(P))
        load("pick", [NPART * 32, NS], w["pick"])
        t["loads"] = loads
        done = {n: ctx.enter_context(nc.semaphore(n)) for n in ("ld1", "dv", "bn1")}
        a = dict(x=x, q_scr=scr["q"], k_scr=scr["k"], ident=w["ident"],
                 bo_bc=w["bo"].partition_broadcast(P), bv_bc=w["bv"].partition_broadcast(P))
        banks = [ctx.enter_context(nc.psum_tensor(f"bank{i}", [P, 512], F32)) for i in range(8)]
        early = early_buffers(sb)
        with ExitStack() as only0:
            start0, last0 = layer0(nc, lambda name, shape, dt=F32: only0.enter_context(
                nc.sbuf_tensor(name, shape, dt)), sem, banks, a, w, t, done)
        all1 = layer1(nc, sb, sem, banks, w, t, early, done, out)
        block = ctx.enter_context(nc.Block())
        for name in ("sync", "tensor", "scalar", "vector", "gpsimd"):
            def run(eng, name=name):
                start0[name](eng)
                all1[name](eng, last0[name])

            {"sync": block.sync, "tensor": block.tensor, "scalar": block.scalar, "vector": block.vector,
             "gpsimd": block.gpsimd}[name](run)


def kernel(**inputs):
    import numpy as _np
    import concourse.bacc as _bacc
    from concourse import mybir as _mybir
    from concourse.bass_utils import run_bass_kernel_spmd as _run

    nc = _bacc.Bacc("TRN2", target_bir_lowering=False, num_devices=1)
    host = {}
    for name, v in inputs.items():
        short = name.split("_", 2)[2]
        v = _np.asarray(v)
        if name.startswith("L1_ffn") and v.ndim == 2:
            short, v = short[:3] + "t", v.T
        elif v.ndim == 1 and v.size > P:
            v = v.reshape(-1, P).T
        elif name in ("L0_ffn_w1", "L0_ffn_w2"):
            short = "e" + short
        host[short] = _np.ascontiguousarray(v)
    host["ident"] = _np.eye(P, dtype=_np.float32)
    host["pick"] = _np.tile(_np.eye(32, NS, dtype=_np.float32), (NPART, 1))
    arrays, w = {}, {}
    for n, v in host.items():
        arrays[f"in_{n}"] = v
        w[n] = nc.dram_tensor(f"in_{n}", v.shape, _mybir.dt.from_np(v.dtype), kind="ExternalInput").ap()
    scr = {n: nc.dram_tensor(f"{n}_scr", (NB, ROWS, h, T), _mybir.dt.bfloat16, kind="Internal").ap()
           for n, h in (("q", NH), ("k", NKV))}
    out = nc.dram_tensor("out", (NB, T, P), _mybir.dt.float32, kind="ExternalOutput").ap()
    program(nc, w, scr, out)
    r = _run(nc, [arrays], core_ids=[0])
    return r.results[0]["out"]
```

```python
from contextlib import ExitStack

import numpy as np

import concourse.bass as bass
from concourse import mybir

F32, BF16 = mybir.dt.float32, mybir.dt.bfloat16
ALU, ACT, AX = mybir.AluOpType, mybir.ActivationFunctionType, mybir.AxisListType

P = 128
NB, T = 8, 256
NT = NB * T // P
TPB = T // P
NH, NKV, HD = 16, 4, 8
G = NH // NKV
NE = 8
DFF = 512
KC = DFF // P
DI = 256
CI = DI // P
NS = 16
TAPS = 4
GT = 512
NG = NB * T // GT
GB = GT // T
GTT = GT // P
LN_EPS = 1e-5
F32_EPS = float(np.finfo(np.float32).eps)
Q_PART = [0, 0, 0, 1, 1, 2]
K_PART = [0, 1, 2, 0, 1, 0]
Q_RUNS = ((0, 3, 0, 0), (3, 5, 1, 1), (5, 6, 2, 3))
K_RUNS = ((5, 6, 0), (3, 5, 0), (0, 3, 0))
NPART = 3
ROWS = HD * len(Q_PART)
MROWS = ROWS + NPART
VW = 32


def reached(eng, sem, b, per, k):
    v = b * per + k
    if isinstance(v, int) and v <= 0:
        return
    eng.wait_ge(sem, v)


def settled(eng, sem, v):
    eng.wait_ge(sem, v)


PE_ORDER = """ffn_in0 probs3 xn_transposes v_gate project S S S ffn_in1 S S ffn_out A tail_heads S A S A S A S
    tail_back A S probs0 A S A S tail_out A A S A S probs1 A A S S A first_heads A A max_rows A
    probs2""".split()
ACT_ORDER = """second_out xn_out relu0 qk_out relu1 gate_exp E E E E E E E E E E E first_out E E E
    negated_maxima E E""".split()
DVE_ORDER = """normalised v_out M M M M M second_heads M M gate_sum M heads_back M M M gate_norm M residual M
    gated M M M first_heads""".split()
POOL_ORDER = """logits qk_split G G G G G G G maxima_split""".split()


PE_LAST = """probs3 x_transposes A A tail_heads A x_in0 A tail_back A x_in1 A probs0 A A tail_out A A probs1
    A A x_in2 A A x_in3 first_heads probs2 A A""".split()
ACT_LAST = """x_deviation second_out E x_out E E x_taps0 E x_taps1 E E E E E E first_out E E E E E E
    x_decay_rates""".split()
DVE_LAST = "x_normalised second_heads heads_back x_conv0 residual x_conv1 first_heads".split()


def run_order(order, pieces, **series):
    count = {letter: 0 for letter in series}
    for name in order:
        if name in series:
            series[name](count[name])
            count[name] += 1
        else:
            pieces[name]()


def layer0(nc, sb, sem, banks, a, w, t, done):
    x_sb, xb_sb = sb("x_sb", [P, NT, P]), sb("xb_sb", [P, NT, P])
    bo_bc, bv_bc = sb("bo_bc", [P, P]), sb("bv_bc", [P, NKV * HD])
    wq, wk4, wv = sb("wq", [P, P]), sb("wk4", [P, 4, NKV * HD]), sb("wv", [P, NKV * HD])
    wo, wg = sb("wo", [P, P]), sb("wg", [P, NE])
    w1, w2 = sb("w1", [P, DFF]), sb("w2", [P, KC, P])
    bq_c, bk_c = sb("bq_c", [P, 1]), sb("bk_c", [P, 1])
    bst, mv = sb("bst", [P, NT, 6]), sb("mv", [P, NT, 2])
    std, rstd = sb("std", [P, NT]), sb("rstd", [P, NT])
    xn = sb("xn", [P, TPB, P])
    xnT = [sb(f"xnT_{p}", [P, T]) for p in range(2)]
    qk = sb("qk", [P, 2 * T])
    qk_rest = sb("qk_rest", [P, 2 * T])
    qk_parts = sb("qk_parts", [P, NPART, 2 * T], BF16)
    q_st = [sb(f"q_st{p}", [MROWS, NH, T], BF16) for p in range(2)]
    k_st = [sb(f"k_st{p}", [MROWS, NKV, T], BF16) for p in range(2)]
    q_sc, k_sc = sb("q_sc", [ROWS, NH, T], BF16), sb("k_sc", [ROWS, NKV, T], BF16)
    v_sb = [sb(f"v_sb{p}", [P, TPB, NKV, VW]) for p in range(2)]
    mx = sb("mx", [P, NH, TPB])
    negm, negm_rest = sb("negm", [TPB * NH, P]), sb("negm_rest", [TPB * NH, P])
    m_parts = sb("m_parts", [TPB * NH, NPART, P], BF16)
    pt = sb("pt", [P, 8, 512])
    o_sb = sb("o_sb", [P, 2, 512])
    on = sb("on", [P, TPB, P])
    rden = sb("rden", [P, 2, 16])
    oT = sb("oT", [P, T])
    hT = sb("hT", [P, KC, T])
    srt, gex = sb("srt", [P, TPB, NE]), sb("gex", [P, TPB, NE])
    gd, g4, g2 = sb("gd", [P, TPB, NE]), sb("g4", [P, TPB, 4]), sb("g2", [P, TPB, 2])
    gz, gp2, gs = sb("gz", [P, TPB, 1]), sb("gp2", [P, TPB, 2]), sb("gs", [P, TPB, 1])
    grz, grm = sb("grz", [P, TPB, 1]), sb("grm", [P, TPB, 1])
    gm, gq, gate = sb("gm", [P, TPB, 1]), sb("gq", [P, TPB, 2]), sb("gate", [P, TPB, 1])
    ident, x1 = t["ident"], t["x1"]

    s_bank, st_bank = banks[0:2], banks[2:4]
    pv_bank = banks[4]
    bA, bB, bC = banks[5:8]

    ld_x0, ld_x, ld_qk, ld_w, ld_row = (sem(n) for n in ("ld_x0", "ld_x", "ld_qk", "ld_w", "ld_row"))
    init_p, xb_ok = sem("init_p"), sem("xb_ok")
    st_bn, st_mv, st_sd, st_rs = sem("st_bn"), sem("st_mv"), sem("st_sd"), sem("st_rs")
    (xn_ok, xnT_ps, xnT_ok, qk_ps, qk_ok, split, scr_ok, sc_ok, stk_ok, mT_ps, negm_ok, msplit, mrow_ok,
     h_ps, h_ok, v_ps, v_ok, srt_ok, gex_ok, gch, f_ps, y_ok, s_ps, mx_ok, st_ps, p_ok, pv_ok,
     o_ok, ot_ps, rd_ok, on_ok, oT_ps, oT_ok, w_ps, x1_ok, gr_ok) = [
        sem(n) for n in (
            "xn_ok", "xnT_ps", "xnT_ok", "qk_ps", "qk_ok", "split", "scr_ok", "sc_ok", "stk_ok", "mT_ps",
            "negm_ok", "msplit", "mrow_ok", "h_ps", "h_ok", "v_ps", "v_ok", "srt_ok", "gex_ok", "gch",
            "f_ps", "y_ok", "s_ps", "mx_ok", "st_ps", "p_ok", "pv_ok", "o_ok", "ot_ps", "rd_ok",
            "on_ok", "oT_ps", "oT_ok", "w_ps", "x1_ok", "gr_ok")]
    FIRST_TILES = ((0, TPB), (TPB, NT))
    NSTK = len(Q_RUNS) + len(K_RUNS)
    NMR = NPART
    NGC = 8

    def steps(body):
        def run(eng, first=-2):
            for i in range(first, 1):
                body(eng, i, i % 2)
            with eng.Fori(1, NB - 4, 2) as i:
                body(eng, i, 1, full=True)
                body(eng, i + 1, 0, full=True)
            for i in range(NB - 3, NB - 1):
                body(eng, i, i % 2)
        return run

    def has(i, off, full):
        return full or 0 <= i + off < NB

    def sync_body(eng, i, par, full=False):
        if has(i, 2, full):
            q_out = a["q_scr"][bass.ds(i + 2, 1)].rearrange("o p c n -> (o p) c n")
            k_out = a["k_scr"][bass.ds(i + 2, 1)].rearrange("o p c n -> (o p) c n")
            for c0, c1, pq, when in Q_RUNS:
                reached(eng, *((qk_ok, i + 2, 1, 1) if when == 0 else (split, i + 2, 3, when)))
                eng.dma_start(q_out[:, c0:c1, :],
                              qk_parts[:, pq:pq + 1, 0:T].broadcast_to([P, c1 - c0, T])).then_inc(scr_ok, 16)
                if when == 0:
                    c0, c1, p0 = K_RUNS[0]
                    eng.dma_start(k_out[:, c0:c1, :], qk_parts[0:NKV * HD, p0:p0 + c1 - c0,
                                                               T:2 * T]).then_inc(scr_ok, 16)
            for c0, c1, p0 in K_RUNS[1:]:
                eng.dma_start(k_out[:, c0:c1, :], qk_parts[0:NKV * HD, p0:p0 + c1 - c0,
                                                           T:2 * T]).then_inc(scr_ok, 16)
        if isinstance(i, int) and i == 0:
            for dst, src in t["loads"]:
                eng.dma_start(dst, src).then_inc(done["ld1"], 16)
        if has(i, 2, full):
            reached(eng, scr_ok, i + 2, 16 * NSTK, 16 * NSTK)
            reached(eng, s_ps, i + 1, NH, NH)
            for dst, src in ((q_sc, q_out), (k_sc, k_out)):
                eng.dma_start(dst[:, :, :], src.rearrange("(h d) c n -> (d c) h n", d=HD)).then_inc(sc_ok, 16)
        if has(i, 1, full):
            for p, when in ((0, 0), (1, 1), (2, 3)):
                reached(eng, *((negm_ok, i + 1, 1, 1) if when == 0 else (msplit, i + 1, 3, when)))
                eng.dma_start(q_st[1 - par][ROWS + p:ROWS + p + 1, :, :].rearrange("o h n -> o (h n)"),
                              m_parts[:, p, :]).then_inc(mrow_ok, 16)
        if has(i, 2, full):
            reached(eng, st_ps, i, NH, NH)
            if isinstance(i, int) and i + 2 < 2:
                eng.wait_ge(init_p, 2)
            for dst, src in ((q_st, q_out), (k_st, k_out)):
                eng.dma_start(dst[par][0:ROWS, :, :],
                              src.rearrange("(h d) c n -> (d c) h n", d=HD)).then_inc(stk_ok, 16)

    def sync_start(eng):
        eng.dma_start(x_sb[:, 0:TPB, :], a["x"][:, 0:TPB, :]).then_inc(ld_x0, 16)
        for dst, src in ((ident[:, :], a["ident"]), (wq[:, :], w["Wq"]), (wk4[:, :, :], a["wk4"])):
            eng.dma_start(dst, src).then_inc(ld_qk, 16)
        for c in range(TPB, NT, NT // 4):
            hi = min(c + NT // 4, NT)
            eng.dma_start(x_sb[:, c:hi, :], a["x"][:, c:hi, :]).then_inc(ld_x, 16)
        for dst, src in ((wv[:, :], w["Wv"]), (wg[:, :], w["Wg"]), (w1[:, :], w["ew1"]),
                         (w2[:, :, :], w["ew2"].rearrange("(k p) n -> p k n", p=P)), (wo[:, :], w["Wo"])):
            eng.dma_start(dst, src).then_inc(ld_w, 16)
        steps(sync_body)(eng)

    def pe_body(eng, i, par, full=False, order=PE_ORDER, extra={}):
        od = 1 - par
        mm = eng.matmul

        def scores(n):
            if not has(i, 1, full):
                return
            q, pair = n // (NH // 2), n % (NH // 2)
            if n == 0:
                reached(eng, sc_ok, i + 1, 32, 32)
            reached(eng, mx_ok, i + 1, NH, n - 1)
            for j in range(2):
                last = mm(s_bank[n % 2][:, j * T:(j + 1) * T],
                          q_sc[:, 2 * pair + j, q * P:(q + 1) * P], k_sc[:, 2 * pair // G, :],
                          start=True, stop=True)
            last.then_inc(s_ps, 1)

        def pv(b_par, b, grp):
            kt = grp % 2
            reached(eng, p_ok, b, NH, 4 * grp + 4)
            if grp == 0:
                reached(eng, o_ok, b, 2, 0)
                reached(eng, v_ok, b, 1, 1)
            if grp == 2:
                reached(eng, o_ok, b, 2, 1)
            for kv in range(NKV):
                last = mm(pv_bank[kv * VW:(kv + 1) * VW, :], v_sb[b_par][:, kt, kv, :],
                          pt[:, (4 * grp + kv) % 8, :], start=(kt == 0), stop=(kt == 1))
            last.then_inc(pv_ok, 1)

        def o_transposes(b, gp, dst):
            reached(eng, o_ok, b, 2, gp + 1)
            for q in range(TPB):
                for g in range(2):
                    c = q * 2 + g
                    last = eng.transpose(dst[:, c * P:(c + 1) * P],
                                         o_sb[:, gp, g * T + q * P:g * T + (q + 1) * P], ident[:, :])
            last.then_inc(ot_ps, 1)

        def ffn_in(half):
            if not has(i, 1, full):
                return
            if half == 0:
                reached(eng, xnT_ok, i + 1, 1, 1)
                reached(eng, on_ok, i - 1, 2, 1)
                reached(eng, y_ok, i, 1, 1)
            else:
                reached(eng, h_ok, i + 1, 2, 1)
            for j in range(2):
                c = 2 * half + j
                last = mm(bB[:, j * T:(j + 1) * T], w1[:, c * P:(c + 1) * P], xnT[od][:, :],
                          start=True, stop=True)
            last.then_inc(h_ps, 1)

        def ffn_out():
            if not has(i, 1, full):
                return
            reached(eng, h_ok, i + 1, 2, 2)
            for q in range(TPB):
                for c in range(KC):
                    last = mm(bB[:, q * P:(q + 1) * P], hT[:, c, q * P:(q + 1) * P], w2[:, c, :],
                              start=(c == 0), stop=(c == KC - 1))
            last.then_inc(f_ps, 1)

        def tail_heads():
            if not has(i, -1, full):
                return
            reached(eng, qk_ok, i + 2 if has(i, 2, full) else NB - 1, 1, 1)
            o_transposes(i - 1, 1, bA)

        def tail_back():
            if not has(i, -1, full):
                return
            reached(eng, on_ok, i - 1, 2, 2)
            nxt = i + 1 if has(i, 1, full) else NB - 1
            reached(eng, v_ok, nxt, 1, 1)
            reached(eng, srt_ok, nxt, 2, 2)
            if has(i, 0, full):
                reached(eng, negm_ok, i, 1, 1)
            for q in range(TPB):
                last = eng.transpose(bC[:, q * P:(q + 1) * P], on[:, q, :], ident[:, :])
            last.then_inc(oT_ps, 1)

        def tail_out():
            if not has(i, -1, full):
                return
            reached(eng, oT_ok, i - 1, 1, 1)
            for q in range(TPB):
                last = mm(bC[:, q * P:(q + 1) * P], oT[:, q * P:(q + 1) * P], wo[:, :],
                          start=True, stop=True)
            last.then_inc(w_ps, 1)

        def max_rows():
            if not has(i, 1, full):
                return
            reached(eng, mx_ok, i + 1, NH, NH)
            reached(eng, v_ok, i + 1, 1, 1)
            reached(eng, srt_ok, i + 1, 2, 2)
            if has(i, -1, full):
                reached(eng, x1_ok, i - 1, 1, 1)
            eng.transpose(bC[0:TPB * NH, 0:P], mx[:, :, :].rearrange("p h q -> p (h q)"),
                          ident[:, :]).then_inc(mT_ps, 1)

        def v_gate():
            if not has(i, 1, full):
                return
            reached(eng, negm_ok, i, 1, 1)
            for q in range(TPB):
                mm(bC[:, q * 32:(q + 1) * 32], xnT[od][:, q * P:(q + 1) * P], wv[:, :],
                   start=True, stop=True)
                last = mm(bC[:, 128 + q * NE:128 + (q + 1) * NE], xnT[od][:, q * P:(q + 1) * P],
                          wg[:, :], start=True, stop=True)
            last.then_inc(v_ps, 1)

        def xn_transposes():
            if not has(i, 2, full):
                return
            reached(eng, xn_ok, i + 2, 1, 1)
            reached(eng, qk_ok, i + 1, 1, 1)
            for q in range(TPB):
                last = eng.transpose(bA[:, q * P:(q + 1) * P], xn[:, q, :], ident[:, :])
            last.then_inc(xnT_ps, 1)

        def project():
            if not has(i, 2, full):
                return
            reached(eng, xnT_ok, i + 2, 1, 1)
            mm(bA[:, 0:T], wq[:, :], xnT[par][:, :], start=True, stop=True)
            mm(bA[:, T:2 * T], wk4[:, :, :].rearrange("p r n -> p (r n)"), xnT[par][:, :],
               start=True, stop=True).then_inc(qk_ps, 1)

        def attend_scores(n):
            if not has(i, 0, full):
                return
            gp, kt, kv = n // 8, n // 4 % 2, n % 4
            if n == 0:
                reached(eng, stk_ok, i, 32, 32)
                reached(eng, mrow_ok, i, 16 * NMR, 16 * NMR)
            reached(eng, p_ok, i, NH, n - 1)
            h0 = kv * G + 2 * gp
            mm(st_bank[n % 2][:, :], k_st[par][:, kv, kt * P:(kt + 1) * P],
               q_st[par][:, h0:h0 + 2, :].rearrange("r h n -> r (h n)"),
               start=True, stop=True).then_inc(st_ps, 1)

        def first_heads():
            if not has(i, 0, full):
                return
            reached(eng, y_ok, i + 1 if has(i, 1, full) else NB - 1, 1, 1)
            o_transposes(i, 0, bB)

        def probs(grp):
            if has(i, 0, full):
                pv(par, i, grp)

        def last_probs():
            if has(i, -1, full):
                pv(od, i - 1, 3)

        run_order(order, dict(
            probs0=lambda: probs(0), probs1=lambda: probs(1), probs2=lambda: probs(2), probs3=last_probs,
            ffn_in0=lambda: ffn_in(0), ffn_in1=lambda: ffn_in(1), ffn_out=ffn_out, v_gate=v_gate,
            xn_transposes=xn_transposes, project=project, tail_heads=tail_heads, tail_back=tail_back,
            tail_out=tail_out, first_heads=first_heads, max_rows=max_rows, **extra), S=scores, A=attend_scores)

    def tensor_start(eng):
        eng.wait_ge(ld_qk, 16 * 3)
        pe_body(eng, -2, 0)
        eng.wait_ge(ld_w, 16 * 5)
        steps(pe_body)(eng, first=-1)

    def act_body(eng, i, par, full=False, order=ACT_ORDER, extra={}):
        od = 1 - par

        def second_out():
            if has(i, -1, full):
                reached(eng, pv_ok, i - 1, 4, 4)
                eng.activation(o_sb[:, 1, :], pv_bank[:, :], ACT.Copy).then_inc(o_ok, 1)

        def xn_out():
            if has(i, 2, full):
                reached(eng, xnT_ps, i + 2, 1, 1)
                reached(eng, f_ps, i, 1, 1)
                reached(eng, v_ps, i, 1, 1)
                eng.activation(xnT[par][:, :], bA[:, 0:T], ACT.Copy).then_inc(xnT_ok, 1)

        def negated_maxima():
            if not has(i, 1, full):
                return
            reached(eng, mT_ps, i + 1, 1, 1)
            reached(eng, msplit, i, 3, 3)
            reached(eng, mrow_ok, i, 16 * NMR, 16 * NMR)
            eng.activation(m_parts[:, 0, :], bC[0:TPB * NH, 0:P], ACT.Copy, scale=-1.0)
            eng.activation(negm[:, :], bC[0:TPB * NH, 0:P], ACT.Copy, scale=-1.0).then_inc(negm_ok, 1)

        def relu(half):
            if has(i, 1, full):
                reached(eng, h_ps, i + 1, 2, half + 1)
                reached(eng, f_ps, i, 1, 1)
                eng.activation(hT[:, 2 * half:2 * half + 2, :],
                               bB[:, :].rearrange("p (c n) -> p c n", c=2), ACT.Relu).then_inc(h_ok, 1)

        def qk_out():
            if not has(i, 2, full):
                return
            reached(eng, qk_ps, i + 2, 1, 1)
            reached(eng, split, i + 1, 3, 3)
            reached(eng, scr_ok, i + 1, 16 * NSTK, 16 * NSTK)
            for half, bias in ((0, bq_c), (1, bk_c)):
                c = slice(half * T, (half + 1) * T)
                eng.activation(qk[:, c], bA[:, c], ACT.Identity, bias=bias[:, 0:1])
                last = eng.activation(qk_parts[:, 0, c], bA[:, c], ACT.Identity, bias=bias[:, 0:1])
            last.then_inc(qk_ok, 1)

        def gate_exp():
            if has(i, 1, full):
                reached(eng, gch, i + 1, NGC, 1)
                reached(eng, gch, i, NGC, NGC)
                eng.activation(gex[:, :, :], gd[:, :, :], ACT.Exp).then_inc(gex_ok, 1)

        def probabilities(n):
            if has(i, 0, full):
                reached(eng, st_ps, i, NH, n + 1)
                if n % 4 == 0:
                    reached(eng, pv_ok, i, 4, n // 4 - 1)
                eng.activation(pt[:, n % 8, :], st_bank[n % 2][:, :], ACT.Exp,
                               scale=HD ** -0.5).then_inc(p_ok, 1)

        def first_out():
            if has(i, 0, full):
                reached(eng, pv_ok, i, 4, 2)
                reached(eng, ot_ps, i - 1, 2, 1)
                eng.activation(o_sb[:, 0, :], pv_bank[:, :], ACT.Copy).then_inc(o_ok, 1)

        run_order(order, dict(
            second_out=second_out, xn_out=xn_out, relu0=lambda: relu(0), relu1=lambda: relu(1),
            qk_out=qk_out, gate_exp=gate_exp, first_out=first_out, negated_maxima=negated_maxima, **extra),
            E=probabilities)

    def scalar_start(eng):
        for dst, src in ((bk_c[:, :], a["bk4"]), (bq_c[:, :], w["bq"].rearrange("(p o) -> p o", o=1)),
                         (bo_bc[:, :], a["bo_bc"]), (bv_bc[:, :], a["bv_bc"])):
            eng.dma_start(dst, src).then_inc(ld_row, 16)
        for part, (lo, hi) in enumerate(FIRST_TILES):
            eng.wait_ge(st_mv, 2 * part + 2)
            eng.activation(std[:, lo:hi], t["veps"][:, lo:hi], ACT.Sqrt).then_inc(st_sd, 1)
            if part == 0:
                eng.wait_ge(ld_row, 16 * 4)
                act_body(eng, -2, 0)
        steps(act_body)(eng, first=-1)

    def dve_body(eng, i, par, full=False, order=DVE_ORDER, extra={}):
        od = 1 - par

        def maxima(n):
            if not has(i, 1, full):
                return
            q, pair = n // (NH // 2), n % (NH // 2)
            reached(eng, s_ps, i + 1, NH, n + 1)
            if n == 0:
                reached(eng, mT_ps, i, 1, 1)
            eng.tensor_reduce(mx[:, 2 * pair:2 * pair + 2, q], s_bank[n % 2][:, :].rearrange("p (h k) -> p h k", h=2),
                              AX.X, ALU.max).then_inc(mx_ok, 1)

        def heads(b, gp, src):
            reached(eng, ot_ps, b, 2, gp + 1)
            v = src[:, :].rearrange("p (q c w) -> p q c w", q=TPB, w=VW)
            r = rden[:, gp, :].rearrange("p (q c o) -> p q c o", q=TPB, o=1)
            eng.reciprocal(r, v[:, :, :, HD:HD + 1]).then_inc(rd_ok, 1)
            reached(eng, rd_ok, b, 2, gp + 1)
            half = on[:, :, gp * P // 2:(gp + 1) * P // 2]
            eng.tensor_tensor(half.rearrange("p q (c d) -> p q c d", d=HD), v[:, :, :, 0:HD],
                              r.broadcast_to([P, TPB, NH // 2, HD]), ALU.mult).then_inc(on_ok, 1)

        def v_out():
            if not has(i, 1, full):
                return
            reached(eng, v_ps, i + 1, 1, 1)
            reached(eng, pv_ok, i - 1, 4, 4)
            reached(eng, gch, i, NGC, 1)
            eng.tensor_tensor(v_sb[od][:, :, :, 0:HD],
                              bC[:, 0:64].rearrange("p (q k d) -> p q k d", q=TPB, k=NKV),
                              bv_bc[:, :].rearrange("p (o k d) -> p o k d", o=1, k=NKV)
                              .broadcast_to([P, TPB, NKV, HD]), ALU.add).then_inc(v_ok, 1)
            for q in range(TPB):
                eng.max(srt[:, q, :], bC[:, 128 + q * NE:128 + (q + 1) * NE]).then_inc(srt_ok, 1)

        def second_heads():
            if has(i, -1, full):
                heads(i - 1, 1, bA)

        def heads_back():
            if has(i, -1, full):
                reached(eng, oT_ps, i - 1, 1, 1)
                eng.tensor_copy(oT[:, :], bC[:, 0:T]).then_inc(oT_ok, 1)

        def residual():
            if not has(i, -1, full):
                return
            reached(eng, w_ps, i - 1, 1, 1)
            reached(eng, y_ok, i - 1, 1, 1)
            tile0 = (i - 1) * TPB
            eng.tensor_tensor(x1[:, bass.ds(tile0, TPB), :], xb_sb[:, bass.ds(tile0, TPB), :],
                              bC[:, 0:T].rearrange("p (q n) -> p q n", q=TPB), ALU.add).then_inc(x1_ok, 1)
            reached(eng, x1_ok, i - 1, 1, 1)
            for q in range(TPB):
                eng.bn_stats(t["bst1"][:, bass.ds(tile0 + q, 1), :].rearrange("p o s -> p (o s)"),
                             x1[:, bass.ds(tile0 + q, 1), :].rearrange("p o n -> p (o n)")
                             ).then_inc(done["bn1"], 1)

        def gate_sum():
            if has(i, 1, full):
                reached(eng, gch, i + 1, NGC, 4)
                eng.reciprocal(grz[:, :, :], gz[:, :, :]).then_inc(gr_ok, 1)

        def gate_norm():
            if has(i, 1, full):
                reached(eng, gch, i + 1, NGC, 6)
                eng.tensor_scalar(gm[:, :, :], gs[:, :, :], F32_EPS, None, ALU.max).then_inc(gr_ok, 1)
                reached(eng, gr_ok, i + 1, 3, 2)
                eng.reciprocal(grm[:, :, :], gm[:, :, :]).then_inc(gr_ok, 1)

        def gated():
            if not has(i, 1, full):
                return
            reached(eng, f_ps, i + 1, 1, 1)
            reached(eng, gch, i + 1, NGC, NGC)
            for q in range(TPB):
                row = xb_sb[:, bass.ds((i + 1) * TPB + q, 1), :].rearrange("p o n -> p (o n)")
                last = eng.scalar_tensor_tensor(row, bB[:, q * P:(q + 1) * P], gate[:, q, 0:1], row,
                                                ALU.mult, ALU.add)
            last.then_inc(y_ok, 1)

        def normalised():
            if not has(i, 3, full):
                return
            reached(eng, xnT_ps, i + 2, 1, 1)
            for q in range(TPB):
                c = (i + 3) * TPB + q
                last = eng.tensor_scalar(xn[:, q, :], x_sb[:, bass.ds(c, 1), :].rearrange("p o n -> p (o n)"),
                                         mv[:, bass.ds(c, 1), 0:1].rearrange("p o s -> p (o s)"),
                                         rstd[:, bass.ds(c, 1)], ALU.subtract, ALU.mult)
            last.then_inc(xn_ok, 1)

        def first_heads():
            if has(i, 0, full):
                heads(i, 0, bB)

        run_order(order, dict(
            v_out=v_out, normalised=normalised, second_heads=second_heads, gate_sum=gate_sum,
            heads_back=heads_back, gate_norm=gate_norm, residual=residual, gated=gated,
            first_heads=first_heads, **extra), M=maxima)

    def vector_start(eng):
        for p in range(2):
            eng.memset(v_sb[p][:, :, :, :], 0.0).then_inc(done["dv"], 1)
        eng.wait_ge(done["dv"], 2)
        for p in range(2):
            eng.memset(v_sb[p][:, :, :, HD:HD + 1], 1.0).then_inc(v_init := done["dv"], 1)
        for part, (lo, hi) in enumerate(FIRST_TILES):
            eng.wait_ge(*((ld_x0, 16) if part == 0 else (ld_x, 16 * 4)))
            for c in range(lo, hi):
                eng.bn_stats(bst[:, c, :], x_sb[:, c, :]).then_inc(st_bn, 1)
            eng.wait_ge(st_bn, hi)
            for c in range(lo, hi):
                last = eng.bn_aggr(mv[:, c, :], bst[:, c, :])
            last.then_inc(st_mv, 1)
            eng.wait_ge(st_mv, 2 * part + 1)
            eng.tensor_scalar(t["veps"][:, lo:hi], mv[:, lo:hi, 1], LN_EPS, None, ALU.add).then_inc(st_mv, 1)
            eng.wait_ge(st_sd, part + 1)
            eng.reciprocal(rstd[:, lo:hi], std[:, lo:hi]).then_inc(st_rs, 1)
            eng.wait_ge(st_rs, part + 1)
            dve_body(eng, part - 3, (part - 3) % 2)
        eng.wait_ge(done["dv"], 4)
        eng.wait_ge(ld_row, 16 * 4)
        eng.wait_ge(xb_ok, 1)
        steps(dve_body)(eng, first=-1)

    def pool_body(eng, i, par, full=False, order=POOL_ORDER, extra={}):
        TT = eng.tensor_tensor

        def logits():
            if has(i, 1, full):
                reached(eng, srt_ok, i + 1, 2, 2)
                reached(eng, gex_ok, i, 1, 1)
                TT(gd[:, :, :], srt[:, :, :], srt[:, :, 0:1].broadcast_to([P, TPB, NE]),
                   ALU.subtract).then_inc(gch, 1)

        def qk_split():
            if has(i, 2, full):
                reached(eng, qk_ok, i + 2, 1, 1)
                TT(qk_parts[:, 1, :], qk[:, :], qk_parts[:, 0, :], ALU.subtract).then_inc(split, 1)
                TT(qk_rest[:, :], qk[:, :], qk_parts[:, 0, :], ALU.subtract).then_inc(split, 1)
                reached(eng, split, i + 2, 3, 2)
                TT(qk_parts[:, 2, :], qk_rest[:, :], qk_parts[:, 1, :], ALU.subtract).then_inc(split, 1)

        def gate_step(k):
            if not has(i, 1, full):
                return
            b = i + 1
            reached(eng, gch, b, NGC, k + 1)
            if k == 0:
                reached(eng, gex_ok, b, 1, 1)
                TT(g4[:, :, :], gex[:, :, 0:4], gex[:, :, 4:8], ALU.add).then_inc(gch, 1)
            if k == 1:
                TT(g2[:, :, :], g4[:, :, 0:2], g4[:, :, 2:4], ALU.add).then_inc(gch, 1)
            if k == 2:
                TT(gz[:, :, :], g2[:, :, 0:1], g2[:, :, 1:2], ALU.add).then_inc(gch, 1)
            if k == 3:
                reached(eng, gr_ok, b, 3, 1)
                TT(gp2[:, :, :], gex[:, :, 0:2], grz[:, :, :].broadcast_to([P, TPB, 2]), ALU.mult).then_inc(gch, 1)
            if k == 4:
                TT(gs[:, :, :], gp2[:, :, 0:1], gp2[:, :, 1:2], ALU.add).then_inc(gch, 1)
            if k == 5:
                reached(eng, gr_ok, b, 3, 3)
                TT(gq[:, :, :], gp2[:, :, :], grm[:, :, :].broadcast_to([P, TPB, 2]), ALU.mult).then_inc(gch, 1)
            if k == 6:
                reached(eng, y_ok, b - 1, 1, 1)
                TT(gate[:, :, :], gq[:, :, 0:1], gq[:, :, 1:2], ALU.add).then_inc(gch, 1)

        def maxima_split():
            if not has(i, 1, full):
                return
            reached(eng, negm_ok, i + 1, 1, 1)
            TT(m_parts[:, 1, :], negm[:, :], m_parts[:, 0, :], ALU.subtract).then_inc(msplit, 1)
            TT(negm_rest[:, :], negm[:, :], m_parts[:, 0, :], ALU.subtract).then_inc(msplit, 1)
            reached(eng, msplit, i + 1, 3, 2)
            TT(m_parts[:, 2, :], negm_rest[:, :], m_parts[:, 1, :], ALU.subtract).then_inc(msplit, 1)

        run_order(order, dict(logits=logits, qk_split=qk_split, maxima_split=maxima_split), G=gate_step)

    def gpsimd_start(eng):
        for p in range(2):
            eng.memset(k_st[p][:, :, :], 1.0).then_inc(init_p, 1)
        pool_body(eng, -2, 0)
        eng.wait_ge(ld_x0, 16)
        eng.wait_ge(ld_x, 16 * 4)
        eng.wait_ge(ld_row, 16 * 4)
        eng.tensor_tensor(xb_sb[:, :, :], x_sb[:, :, :],
                          bo_bc[:, :].rearrange("p (o n) -> p o n", o=1).broadcast_to([P, NT, P]),
                          ALU.add).then_inc(xb_ok, 1)
        steps(pool_body)(eng, first=-1)

    bodies = dict(sync=sync_body, tensor=pe_body, scalar=act_body, vector=dve_body, gpsimd=pool_body)
    starts = dict(sync=sync_start, tensor=tensor_start, scalar=scalar_start, vector=vector_start,
                  gpsimd=gpsimd_start)
    return starts, {n: (lambda eng, i, body=body, **kw: body(eng, i, i % 2, **kw)) for n, body in bodies.items()}


def early_buffers(sb):
    n_tok = NB * T
    return dict(
        mv1=sb("mv1", [P, NT, 2]), std1=sb("std1", [P, NT]), rstd1=sb("rstd1", [P, NT]),
        w3s=sb("w3s", [P, KC, P]),
        nega=sb("nega", [P, CI, NS]),
        wx_p=sb("wx_p", [P, CI, NPART * 32]),
        sel=sb("sel", [NPART * 32, NS, P], BF16),
        xn1=sb("xn1", [P, NT, P]), xnT1=sb("xnT1", [P, n_tok]),
        xc=sb("xc", [P, CI, GT]),
        xs=sb("xs", [P, CI, n_tok]), zs=sb("zs", [P, CI, n_tok]))


def layer1(nc, sb, sem, banks, w, t, early, done, out):
    NTOK = NB * T
    x1, ident, bst1 = t["x1"], t["ident"], t["bst1"]
    (win, wdt, wx, wout, w1, w2, h1, h2, w3) = (t[n] for n in
        ("win", "wdt", "wx", "wout", "f1", "f2", "fh1", "fh2", "f3"))
    mv, std, rstd, w3s, nega, wx_p, sel, xn, xnT, xc, xs, zs = (early[n] for n in
        ("mv1", "std1", "rstd1", "w3s", "nega", "wx_p", "sel", "xn1", "xnT1", "xc", "xs", "zs"))
    sil = sb("sil", [P, KC, GT])
    g2 = sb("gelu2", [P, KC, GT])
    g3 = sb("gelu3", [P, KC, GT])
    dt = sb("dt", [P, CI, GT])
    u_abs, u_pos = sb("u_abs", [P, CI, GT]), sb("u_pos", [P, CI, GT])
    e_sb, l_sb = sb("e_sb", [P, CI, GT]), sb("l_sb", [P, CI, GT])
    b_full, b_rest = sb("b_full", [NPART * 32, GT]), sb("b_rest", [NPART * 32, GT])
    b_mid = sb("b_mid", [NPART * 32, GT], BF16)
    b_parts = sb("b_parts", [NPART * 32, NTOK], BF16)
    NR, NRD = 8, 16
    da = sb("da", [P, NRD, GB, T])
    hb = sb("hb", [P, NR, GT])
    acc = sb("acc", [P, CI, GT])
    y = sb("y", [P, CI, GT])

    pA, pB = banks[0:2]
    f_bank = [banks[6], banks[2], banks[3], banks[5]]
    b_bank = [banks[4], banks[7]]

    (i_act, da_zero, st_ok, sd_ok, i_pool, xn_ok, xT_ps, xT_ok, l1_ps, sil_ok, h0_ok, win_ps, z_ok, cv_ok, conv, xs_ok,
     dt_ps, u_ok, sp_ok, spd, bx_ps, bx_ok, bsp, b_ps, da_ok, scan, acc0, acc1, y_ok, l2_ps, g2_ok,
     l3_ps, g3_ok, o_ps, o_ok, out_ok, acc1_0) = [sem("b_" + n) for n in (
         "i_act", "da_zero", "st_ok", "sd_ok", "i_pool", "xn_ok", "xT_ps", "xT_ok", "l1_ps", "sil_ok", "h0_ok", "win_ps",
         "z_ok", "cv_ok", "conv", "xs_ok", "dt_ps", "u_ok", "sp_ok", "spd", "bx_ps", "bx_ok", "bsp",
         "b_ps", "da_ok", "scan", "acc0", "acc1", "y_ok", "l2_ps", "g2_ok", "l3_ps", "g3_ok", "o_ps",
         "o_ok", "out_ok", "acc1_0")]
    NSP = 4
    NPI = 6
    PARTS = ((0, GTT), (GTT, NT))

    def steps(body):
        def run(eng, step0):
            body(eng, -1, between=step0)
            body(eng, 0)
            with eng.Fori(1, NG - 1) as g:
                body(eng, g, full=True)
            body(eng, NG - 1)
            body(eng, NG)
        return run

    def has(g, off, full):
        return full or 0 <= g + off < NG

    def cols(g):
        return bass.ds(g * GT, GT)

    def sync_body(eng, g, full=False, between=None):
        if between:
            between(eng, NB - 1)
            between(eng, NB)
        if has(g, -1, full):
            reached(eng, o_ok, g - 1, 1, 1)
            eng.dma_start(out[:, bass.ds((g - 1) * GTT, GTT), :],
                          x1[:, bass.ds((g - 1) * GTT, GTT), :]).then_inc(out_ok, 16)

    def sync_all(eng, step0):
        steps(sync_body)(eng, step0)
        eng.wait_ge(out_ok, 16 * NG)

    def pe_body(eng, g, full=False, between=None):
        mm = eng.matmul
        nx, cur, prv = has(g, 1, full), has(g, 0, full), has(g, -1, full)
        state = [0]

        def b_row(keep=False):
            s = state[0]
            if not cur or s >= NS:
                return
            state[0] += 1
            if s == 0:
                reached(eng, bsp, g, 4, 4)
            reached(eng, scan, g, 2 * NS, 2 * (s - 1))
            mm(b_bank[s % 2][:, :], sel[:, s, :], b_parts[:, cols(g)], start=True,
               stop=True).then_inc(b_ps, 1)

        def ffn1(c):
            if not cur:
                return
            fa, fb = f_bank[2 * (c % 2)], f_bank[2 * (c % 2) + 1]
            if c < 2:
                reached(eng, g3_ok, g - 1, KC, 2 * c + 2)
                reached(eng, xT_ok, g, 1, 1)
                if isinstance(g, int) and g == 0:
                    eng.wait_ge(xT_ok, 2 * c + 2)
            else:
                reached(eng, h0_ok, g, KC, c - 1)
            mm(fa[:, :], w1[:, c * P:(c + 1) * P], xnT[:, cols(g)], start=True, stop=True)
            mm(fb[:, :], w2[:, c * P:(c + 1) * P], xnT[:, cols(g)], start=True, stop=True).then_inc(l1_ps, 1)

        def w_in(c, dst):
            if nx:
                mm(dst[:, :], win[:, c * P:(c + 1) * P], xnT[:, cols(g + 1)], start=True,
                   stop=True).then_inc(win_ps, 1)

        def hidden(c, wt, src, ready, free, done_sem):
            if not cur:
                return
            for k in range(KC):
                reached(eng, ready, g, KC, k + 1)
                if k == 0:
                    reached(eng, *free)
                last = mm(f_bank[c][:, :], wt[:, k, c * P:(c + 1) * P], src[:, k, :],
                          start=(k == 0), stop=(k == KC - 1))
                if k % 2:
                    b_row() if k < KC - 1 else None
            last.then_inc(done_sem, 1)
            b_row()

        def transposes(b, dst):
            eng.wait_ge(xn_ok, b + 1)
            for q in range(GTT):
                last = eng.transpose(dst[:, q * P:(q + 1) * P], xn[:, b * GTT + q, :], ident[:, :])
            last.then_inc(xT_ps, 1)

        def x_in(c):
            if nx:
                if c == 0:
                    reached(eng, u_ok, g, 4, 4)
                    reached(eng, xT_ok, g + 1, 1, 1)
                if c == 2:
                    reached(eng, conv, g + 1, 6, 3)
                if c == 3:
                    reached(eng, conv, g + 1, 6, 6)
                w_in(c, (pB, pA)[c % 2])

        if between:
            pieces = {f"x_in{c}": (lambda c=c: x_in(c)) for c in range(4)}
            pieces["x_transposes"] = lambda: transposes(0, pA)
            between(eng, NB - 1, order=PE_LAST, extra=pieces)
            between(eng, NB)
            eng.wait_ge(i_pool, NPI)
        ffn1(0)
        ffn1(1)
        if not between:
            x_in(0)
            x_in(1)
        ffn1(2)
        ffn1(3)
        if not between:
            x_in(2)
        b_row()
        b_row()
        if not between:
            x_in(3)
        if prv:
            if nx:
                reached(eng, z_ok, g + 1, 2, 1)
            else:
                reached(eng, u_ok, NG - 1, 4, 4)
            reached(eng, y_ok, g - 1, 2, 2)
            reached(eng, g3_ok, g - 1, KC, KC)
            for q in range(GTT):
                r = slice(q * P, (q + 1) * P)
                for k in range(KC):
                    mm(pB[:, r], g3[:, k, r], w3s[:, k, :], start=(k == 0), stop=False)
                for c in range(CI):
                    last = mm(pB[:, r], y[:, c, r], wout[:, c, :], start=False, stop=(c == CI - 1))
            last.then_inc(o_ps, 1)

        def second(c):
            hidden(c, h1, sil, h0_ok, (h0_ok, g, KC, 3 if c < 2 else 4), l2_ps)

        if nx:
            reached(eng, xs_ok, g + 1, 2, 2)
            reached(eng, z_ok, g + 1, 2, 2)
            for c in range(CI):
                last = mm(pA[0:NPART * 32, :], wx_p[:, c, :], xs[:, c, cols(g + 1)],
                          start=(c == 0), stop=(c == CI - 1))
            last.then_inc(bx_ps, 1)
        b_row()
        second(0)
        second(1)

        def step_in(c, dst, *free):
            if nx:
                reached(eng, *free)
                for k in range(CI):
                    last = mm(dst[:, :], wdt[:, k, c * P:(c + 1) * P], xs[:, k, cols(g + 1)],
                              start=(k == 0), stop=(k == CI - 1))
                last.then_inc(dt_ps, 1)
            b_row()

        step_in(0, pA, bx_ok, g + 1, 1, 1)
        second(2)
        step_in(1, pB, o_ok, g - 1, 1, 1)
        second(3)
        if between:
            for b in range(1, NG):
                transposes(b, f_bank[b])
        for c in range(KC):
            hidden(c, h2, g2, g2_ok, (g2_ok, g, KC, c + 1), l3_ps)
        while cur and state[0] < NS:
            b_row()

    def tensor_all(eng, step0):
        eng.wait_ge(done["ld1"], 16 * len(t["loads"]))
        steps(pe_body)(eng, step0)

    def deviation(eng, part):
        lo, hi = PARTS[part]
        eng.wait_ge(st_ok, 3 * part + 2)
        eng.activation(std[:, lo:hi], t["veps"][:, lo:hi], ACT.Sqrt).then_inc(sd_ok, 1)

    def act_body(eng, g, full=False, between=None):
        nx, cur, prv = has(g, 1, full), has(g, 0, full), has(g, -1, full)
        act = eng.activation
        def ffn_silu(c):
            if cur:
                reached(eng, l1_ps, g, KC, c + 1)
                reached(eng, l2_ps, g - 1, KC, KC)
                act(sil[:, c, :], f_bank[2 * (c % 2)][:, :], ACT.Silu,
                    scale=t["f1s"][:, c:c + 1]).then_inc(sil_ok, 1)

        def taps(c, src):
            reached(eng, win_ps, g + 1, 4, c + 1)
            reached(eng, xs_ok, g, 2, 2)
            act(xc[:, c, :], src[:, :], ACT.Identity, bias=t["cb"][:, c:c + 1],
                scale=t["cw"][:, c, TAPS - 1:TAPS]).then_inc(cv_ok, 1)

        def gate_z(c, src):
            reached(eng, win_ps, g + 1, 4, c + 3)
            settled(eng, i_pool, NPI)
            act(zs[:, c, cols(g + 1)], src[:, :], ACT.Silu).then_inc(z_ok, 1)

        def gate_x(c):
            reached(eng, conv, g + 1, 6, 3 * c + 3)
            settled(eng, i_pool, NPI)
            act(xs[:, c, cols(g + 1)], xc[:, c, :], ACT.Silu).then_inc(xs_ok, 1)

        def xnt_out(b, src):
            eng.wait_ge(xT_ps, b + 1)
            act(xnT[:, b * GT:(b + 1) * GT], src[:, :], ACT.Copy).then_inc(xT_ok, 1)

        def decay_rates():
            act(nega[:, :, :], t["alog"][:, :, :], ACT.Exp).then_inc(i_act, 1)
            eng.wait_ge(i_act, 1)
            act(nega[:, :, :], nega[:, :, :], ACT.Copy, scale=-1.0).then_inc(i_act, 1)
            eng.wait_ge(i_act, 2)

        if between:
            between(eng, NB - 1, order=ACT_LAST, extra=dict(
                x_deviation=lambda: deviation(eng, 0), x_out=lambda: xnt_out(0, pA),
                x_taps0=lambda: taps(0, pB), x_taps1=lambda: taps(1, pA), x_decay_rates=decay_rates))
            between(eng, NB)
            eng.wait_ge(i_pool, NPI)
        ffn_silu(0)
        ffn_silu(1)
        if nx and not between:
            taps(0, pB)
            taps(1, pA)
        ffn_silu(2)
        ffn_silu(3)
        if nx:
            gate_x(0)
            gate_z(0, pB)
            gate_x(1)
            gate_z(1, pA)
        if between:
            eng.wait_ge(done["bn1"], NT)
            deviation(eng, 1)

        def decay(s):
            if not cur:
                return
            if s == 0:
                reached(eng, spd, g, NSP, NSP)
            for c in range(CI):
                n = CI * s + c
                reached(eng, scan, g, 2 * NS, n + 1 - NRD)
                act(da[:, n % NRD, :, 1:T],
                    dt[:, c, :].rearrange("p (b n) -> p b n", b=GB)[:, :, 1:T],
                    ACT.Exp, scale=nega[:, c, s:s + 1]).then_inc(da_ok, 1)

        def dt_in(c, src):
            if nx:
                reached(eng, dt_ps, g + 1, 2, c + 1)
                reached(eng, spd, g, NSP, NSP)
                act(u_abs[:, c, :], src[:, :], ACT.Abs, bias=t["bdt"][:, c:c + 1]).then_inc(u_ok, 1)
                act(u_pos[:, c, :], src[:, :], ACT.Relu, bias=t["bdt"][:, c:c + 1]).then_inc(u_ok, 1)

        def b_in():
            if nx:
                reached(eng, bx_ps, g + 1, 1, 1)
                reached(eng, bsp, g, 4, 4)
                settled(eng, i_pool, NPI)
                act(b_parts[:, cols(g + 1)], pA[0:NPART * 32, :], ACT.Copy)
                act(b_full[:, :], pA[0:NPART * 32, :], ACT.Copy).then_inc(bx_ok, 1)

        for s in range(NS):
            decay(s)
            if s == 8:
                b_in()
        dt_in(0, pA)
        dt_in(1, pB)
        if between:
            for b in range(1, NG):
                xnt_out(b, f_bank[b])
        if cur:
            for c in range(KC):
                reached(eng, l2_ps, g, KC, c + 1)
                reached(eng, l3_ps, g - 1, KC, KC)
                act(g2[:, c, :], f_bank[c][:, :], ACT.Gelu, scale=t["h1s"][:, c:c + 1]).then_inc(g2_ok, 1)
        if nx:
            reached(eng, u_ok, g + 1, 4, 4)
            act(e_sb[:, :, :], u_abs[:, :, :], ACT.Exp, scale=-1.0).then_inc(sp_ok, 1)
            reached(eng, spd, g + 1, NSP, 1)
            act(l_sb[:, :, :], u_abs[:, :, :], ACT.Ln).then_inc(sp_ok, 1)
        if cur:
            for c in range(KC):
                reached(eng, l3_ps, g, KC, c + 1)
                reached(eng, o_ps, g - 1, 1, 1)
                act(g3[:, c, :], f_bank[c][:, :], ACT.Gelu, scale=t["h2s"][:, c:c + 1]).then_inc(g3_ok, 1)

    def scalar_all(eng, step0):
        eng.wait_ge(done["ld1"], 16 * len(t["loads"]))
        steps(act_body)(eng, step0)

    def dve_body(eng, g, full=False, between=None):
        nx, cur, prv = has(g, 1, full), has(g, 0, full), has(g, -1, full)
        STT = eng.scalar_tensor_tensor

        def ffn_mul(c):
            if cur:
                reached(eng, sil_ok, g, KC, c + 1)
                STT(sil[:, c, :], f_bank[2 * (c % 2) + 1][:, :], t["f2s"][:, c:c + 1], sil[:, c, :],
                    ALU.mult, ALU.mult).then_inc(h0_ok, 1)

        def other_taps(c, src):
            acc_v = xc[:, c, :].rearrange("p (b n) -> p b n", b=GB)
            src_v = src[:, :].rearrange("p (b n) -> p b n", b=GB)
            reached(eng, cv_ok, g + 1, 2, c + 1)
            for k in range(1, TAPS):
                if k > 1:
                    reached(eng, conv, g + 1, 6, 3 * c + k - 1)
                STT(acc_v[:, :, k:T], src_v[:, :, 0:T - k], t["cw"][:, c, TAPS - 1 - k:TAPS - k],
                    acc_v[:, :, k:T], ALU.mult, ALU.add).then_inc(conv, 1)

        def first_group():
            statistics(eng, 0)
            normalise(eng, 0)

        if between:
            between(eng, NB - 1, order=DVE_LAST, extra=dict(
                x_normalised=first_group, x_conv0=lambda: other_taps(0, pB), x_conv1=lambda: other_taps(1, pA)))
            between(eng, NB)
            eng.memset(da[:, :, :, 0:1], 0.0).then_inc(da_zero, 1)
            eng.wait_ge(da_zero, 1)
            statistics(eng, 1)
            eng.wait_ge(i_pool, NPI)
            for b in range(1, NG):
                normalise(eng, b)
        ffn_mul(0)
        ffn_mul(1)
        for c, src in ((0, pB), (1, pA)):
            if nx and not between:
                other_taps(c, src)
        ffn_mul(2)
        ffn_mul(3)
        for s in range(NS):
            if cur:
                reached(eng, b_ps, g, NS, s + 1)
                for c in range(CI):
                    n = CI * s + c
                    reached(eng, da_ok, g, 2 * NS, n + 1)
                    if c == 1:
                        reached(eng, acc1, g, NS - 1, s - NR // CI)
                    eng.tensor_tensor_scan(hb[:, n % NR, :],
                                           da[:, n % NRD, :, :].rearrange("p b n -> p (b n)"),
                                           b_bank[s % 2][:, :], 0.0, ALU.mult, ALU.add).then_inc(scan, 1)
                if s == 0:
                    reached(eng, scan, g, 2 * NS, 2)
                    for c in range(CI):
                        reached(eng, y_ok, g - 1, 2, c + 1)
                        STT(acc[:, c, :], xs[:, c, cols(g)], t["D"][:, c:c + 1], hb[:, c, :],
                            ALU.mult, ALU.add).then_inc((acc0, acc1_0)[c], 1)
                else:
                    reached(eng, scan, g, 2 * NS, 2 * s + 1)
                    reached(eng, acc0, g, NS, s)
                    eng.tensor_tensor(acc[:, 0, :], acc[:, 0, :], hb[:, CI * s % NR, :],
                                      ALU.add).then_inc(acc0, 1)
            if s == 3 and prv:
                reached(eng, o_ps, g - 1, 1, 1)
                group = x1[:, bass.ds((g - 1) * GTT, GTT), :]
                eng.tensor_tensor(group, group,
                                  pB[:, :].rearrange("p (q n) -> p q n", q=GTT), ALU.add).then_inc(o_ok, 1)
        if nx:
            mid, top = slice(32, 64), slice(64, 96)
            reached(eng, bsp, g + 1, 4, 2)
            eng.tensor_copy(b_parts[mid, cols(g + 1)], b_mid[mid, :]).then_inc(bsp, 1)
            eng.tensor_tensor(b_parts[top, cols(g + 1)], b_rest[top, :], b_mid[top, :],
                              ALU.subtract).then_inc(bsp, 1)
        if nx:
            reached(eng, sp_ok, g + 1, 2, 1)
            eng.tensor_scalar(u_abs[:, :, :], e_sb[:, :, :], 1.0, None, ALU.add).then_inc(spd, 1)
            reached(eng, spd, g + 1, NSP, 1)
            STT(e_sb[:, :, :], u_abs[:, :, :], -1.0, e_sb[:, :, :], ALU.add, ALU.subtract).then_inc(spd, 1)
            reached(eng, spd, g + 1, NSP, 2)
            eng.tensor_tensor(e_sb[:, :, :], u_pos[:, :, :], e_sb[:, :, :], ALU.subtract).then_inc(spd, 1)
            reached(eng, spd, g + 1, NSP, 3)
            reached(eng, sp_ok, g + 1, 2, 2)
            eng.tensor_tensor(dt[:, :, :], e_sb[:, :, :], l_sb[:, :, :], ALU.add).then_inc(spd, 1)
        if cur:
            for c in range(CI):
                reached(eng, acc0 if c == 0 else acc1, g, NS - c, NS - c)
                reached(eng, o_ps, g - 1, 1, 1)
                eng.tensor_tensor(y[:, c, :], acc[:, c, :], zs[:, c, cols(g)], ALU.mult).then_inc(y_ok, 1)

    def normalise(eng, g):
        for c in range(g * GTT, (g + 1) * GTT):
            last = eng.tensor_scalar(xn[:, c, :], x1[:, c, :], mv[:, c, 0:1], rstd[:, c:c + 1],
                                     ALU.subtract, ALU.mult)
        last.then_inc(xn_ok, 1)

    def statistics(eng, part):
        lo, hi = PARTS[part]
        eng.wait_ge(done["bn1"], hi)
        for c in range(lo, hi):
            last = eng.bn_aggr(mv[:, c, :], bst1[:, c, :])
        last.then_inc(st_ok, 1)
        eng.wait_ge(st_ok, 3 * part + 1)
        eng.tensor_scalar(t["veps"][:, lo:hi], mv[:, lo:hi, 1], LN_EPS, None, ALU.add).then_inc(st_ok, 1)
        eng.wait_ge(sd_ok, part + 1)
        eng.reciprocal(rstd[:, lo:hi], std[:, lo:hi]).then_inc(st_ok, 1)
        eng.wait_ge(st_ok, 3 * part + 3)

    def vector_all(eng, step0):
        steps(dve_body)(eng, step0)

    def pool_body(eng, g, full=False, between=None):
        TT = eng.tensor_tensor
        if between:
            between(eng, NB - 1)
            between(eng, NB)
        if has(g, 0, full):
            for s in range(1, NS):
                reached(eng, scan, g, 2 * NS, 2 * s + 2)
                if s == 1:
                    reached(eng, acc1_0, g, 1, 1)
                else:
                    reached(eng, acc1, g, NS - 1, s - 1)
                TT(acc[:, 1, :], acc[:, 1, :], hb[:, (CI * s + 1) % NR, :], ALU.add).then_inc(acc1, 1)
                if s == 10:
                    parts(eng, g + 1, has(g, 1, full))
        else:
            parts(eng, g + 1, has(g, 1, full))

    def parts(eng, g, on):
        if not on:
            return
        TT = eng.tensor_tensor
        reached(eng, bx_ok, g, 1, 1)
        settled(eng, i_pool, NPI)
        TT(b_rest[:, :], b_full[:, :], b_parts[:, cols(g)], ALU.subtract).then_inc(bsp, 1)
        TT(b_mid[:, :], b_full[:, :], b_parts[:, cols(g)], ALU.subtract).then_inc(bsp, 1)

    def gpsimd_all(eng, step0):
        eng.wait_ge(done["ld1"], 16 * len(t["loads"]))
        eng.memset(wx_p[:, :, :], 0.0).then_inc(i_pool, 1)
        eng.wait_ge(i_pool, 1)
        for p in range(NPART):
            eng.tensor_copy(wx_p[:, :, 32 * p:32 * p + NS], wx[:, :, :]).then_inc(i_pool, 1)
        eng.tensor_copy(sel[:, :, :], t["pick"][:, :].rearrange("p (s o) -> p s o", o=1)
                        .broadcast_to([NPART * 32, NS, P])).then_inc(i_pool, 1)
        eng.tensor_tensor(w3s[:, :, :], w3[:, :, :],
                          t["w3s_bc"][:, :].rearrange("p (o n) -> p o n", o=1).broadcast_to([P, KC, P]),
                          ALU.mult).then_inc(i_pool, 1)
        steps(pool_body)(eng, step0)

    return dict(sync=sync_all, tensor=tensor_all, scalar=scalar_all, vector=vector_all, gpsimd=gpsimd_all)


def program(nc, w, scr, out):
    x = w["x"].rearrange("b (q p) d -> p (b q) d", p=P)
    out = out.rearrange("b (q p) d -> p (b q) d", p=P)
    ctx = ExitStack()
    with ctx:
        def sb(name, shape, dt=F32):
            return ctx.enter_context(nc.sbuf_tensor(name, shape, dt))

        def sem(name):
            return ctx.enter_context(nc.semaphore(name))

        t = dict(ident=sb("ident", [P, P]), x1=sb("x1", [P, NT, P]), veps=sb("veps", [P, NT]),
                 bst1=sb("bst1", [P, NT, 6]))
        loads = []

        def load(name, shape, src):
            t[name] = sb("ld_" + name, shape)
            loads.append((t[name][tuple(slice(None) for _ in shape)], src))

        chunks = "(k p) n -> p k n"
        load("win", [P, 2 * DI], w["W_in"])
        load("wdt", [P, CI, DI], w["W_dt"].rearrange(chunks, p=P))
        load("wx", [P, CI, NS], w["W_x"].rearrange(chunks, p=P))
        load("wout", [P, CI, P], w["W_out"].rearrange(chunks, p=P))
        load("cw", [P, CI, TAPS], w["conv_w"].rearrange("(k p) o n -> p k (o n)", p=P))
        load("cb", [P, CI], w["conv_b"])
        load("alog", [P, CI, NS], w["A_log"].rearrange(chunks, p=P))
        load("D", [P, CI], w["D"])
        load("bdt", [P, CI], w["b_dt"])
        load("f1", [P, DFF], w["w1_t"])
        load("f2", [P, DFF], w["w2_t"])
        load("fh1", [P, KC, DFF], w["h1_t"].rearrange(chunks, p=P))
        load("fh2", [P, KC, DFF], w["h2_t"].rearrange(chunks, p=P))
        load("f3", [P, KC, P], w["w3_t"].rearrange(chunks, p=P))
        for n in ("w1", "w2", "h1", "h2"):
            load({"w1": "f1s", "w2": "f2s", "h1": "h1s", "h2": "h2s"}[n], [P, KC], w[n + "_s"])
        load("w3s_bc", [P, P], w["w3_s"].partition_broadcast(P))
        load("pick", [NPART * 32, NS], w["pick"])
        t["loads"] = loads
        done = {n: ctx.enter_context(nc.semaphore(n)) for n in ("ld1", "dv", "bn1")}
        a = dict(x=x, q_scr=scr["q"], k_scr=scr["k"], ident=w["ident"],
                 bo_bc=w["bo"].partition_broadcast(P),
                 wk4=w["Wk"].rearrange("p (o n) -> p o n", o=1).broadcast_to([P, 4, NKV * HD]),
                 bk4=w["bk"].rearrange("(o p q) -> o p q", o=1, q=1).broadcast_to([4, NKV * HD, 1]),
                 bv_bc=w["bv"].partition_broadcast(P))
        banks = [ctx.enter_context(nc.psum_tensor(f"bank{i}", [P, 512], F32)) for i in range(8)]
        early = early_buffers(sb)
        with ExitStack() as only0:
            start0, step0 = layer0(nc, lambda name, shape, dt=F32: only0.enter_context(
                nc.sbuf_tensor(name, shape, dt)), sem, banks, a, w, t, done)
        all1 = layer1(nc, sb, sem, banks, w, t, early, done, out)
        block = ctx.enter_context(nc.Block())
        for name in ("sync", "tensor", "scalar", "vector", "gpsimd"):
            def run(eng, name=name):
                start0[name](eng)
                all1[name](eng, step0[name])

            {"sync": block.sync, "tensor": block.tensor, "scalar": block.scalar, "vector": block.vector,
             "gpsimd": block.gpsimd}[name](run)


def kernel(**inputs):
    import numpy as _np
    import concourse.bacc as _bacc
    from concourse import mybir as _mybir
    from concourse.bass_utils import run_bass_kernel_spmd as _run

    nc = _bacc.Bacc("TRN2", target_bir_lowering=False, num_devices=1)
    host = {}
    for name, v in inputs.items():
        short = name.split("_", 2)[2]
        v = _np.asarray(v)
        if name.startswith("L1_ffn") and v.ndim == 2:
            short, v = short[:3] + "t", v.T
        elif v.ndim == 1 and v.size > P:
            v = v.reshape(-1, P).T
        elif name in ("L0_ffn_w1", "L0_ffn_w2"):
            short = "e" + short
        host[short] = _np.ascontiguousarray(v)
    host["ident"] = _np.eye(P, dtype=_np.float32)
    host["pick"] = _np.tile(_np.eye(32, NS, dtype=_np.float32), (NPART, 1))
    arrays, w = {}, {}
    for n, v in host.items():
        arrays[f"in_{n}"] = v
        w[n] = nc.dram_tensor(f"in_{n}", v.shape, _mybir.dt.from_np(v.dtype), kind="ExternalInput").ap()
    scr = {n: nc.dram_tensor(f"{n}_scr", (NB, h * HD, len(Q_PART), T), _mybir.dt.bfloat16, kind="Internal").ap()
           for n, h in (("q", NH), ("k", NKV))}
    out = nc.dram_tensor("out", (NB, T, P), _mybir.dt.float32, kind="ExternalOutput").ap()
    program(nc, w, scr, out)
    r = _run(nc, [arrays], core_ids=[0])
    return r.results[0]["out"]
```
